# Optimizing a Trainium2 kernel written in Bass

```python
import numpy as np
import jax
import jax.numpy as jnp

def _softmax(x, axis=-1):
    return jax.nn.softmax(x, axis=axis)

def _gelu(x):
    return jax.nn.gelu(x, approximate=True)

def _silu(x):
    return jax.nn.silu(x)

def _sigmoid(x):
    return jax.nn.sigmoid(x)

def _layernorm(x, axis=-1, eps=1e-05):
    m = jnp.mean(x, axis=axis, keepdims=True)
    v = jnp.var(x, axis=axis, keepdims=True)
    return (x - m) / jnp.sqrt(v + eps)

def _scatter_add(tgt, idx, src, axis=0):
    return tgt.at[idx].add(src)

def _segment_sum(src, seg, n):
    return jax.ops.segment_sum(src, seg, n)
kernel_name = 'mk_gnn_preln_d4_gnn_r8_101bf7'

def setup_inputs(seed: int=0):
    np.random.seed(seed)
    _w = jnp.asarray

    def _rec_inputs():
        import jax
        import jax.numpy as jnp
        _gk = jax.random.key(seed)
        x = 1.712e-05 + 0.1 * jax.random.normal(jax.random.fold_in(_gk, 1), (12500, 16), jnp.float32)
        src = jax.random.randint(jax.random.fold_in(_gk, 2), (400000,), 0, 12500, jnp.int32)
        dst = jnp.minimum((12500 * jax.random.uniform(jax.random.fold_in(_gk, 3), (400000,)) ** 2.0).astype(jnp.int32), 99999)
        _o = jnp.argsort(dst, stable=True)
        src = src[_o]
        dst = dst[_o]
        edge_attr_16 = 0.000254407 + 0.99978 * jax.random.normal(jax.random.fold_in(_gk, 13), (400000, 16), jnp.float32)
        edge_attr_8 = -5.3897e-05 + 0.999841 * jax.random.normal(jax.random.fold_in(_gk, 14), (400000, 8), jnp.float32)
        edge_type_230 = jax.random.randint(jax.random.fold_in(_gk, 16), (400000,), 0, 230, jnp.int32)
        node_vec1 = -0.00472126 + 0.997171 * jax.random.normal(jax.random.fold_in(_gk, 17), (12500, 1), jnp.float32)
        return (x, src, dst, edge_attr_16, edge_attr_8, edge_type_230, node_vec1)
    x, src, dst, edge_attr_16, edge_attr_8, edge_type_230, node_vec1 = _rec_inputs()

    def _L0_gnn_setup():
        import jax, jax.numpy as jnp
        import numpy as np
        C = 0.01
        EPS = 1e-06
        MIN_NORM = 1e-10
        BALL_EPS = 1e-05

        def _norm(x):
            return jnp.sqrt(jnp.clip(jnp.sum(x * x, axis=-1, keepdims=True), MIN_NORM))

        def log_map_zero(x, c):
            sc = jnp.sqrt(c)
            n = _norm(x)
            return jnp.arctanh(jnp.clip(sc * n, -1.0 + BALL_EPS, 1.0 - BALL_EPS)) * x / (sc * n)

        def exp_map_zero(v, c):
            sc = jnp.sqrt(c)
            n = _norm(v)
            return jnp.tanh(sc * n) * v / (sc * n)

        def project_to_ball(x, c):
            n = _norm(x)
            maxn = (1.0 - BALL_EPS) / jnp.sqrt(c)
            return jnp.where(n > maxn, x * (maxn / n), x)

        def mobius_add(x, y, c):
            x2 = jnp.sum(x * x, axis=-1, keepdims=True)
            y2 = jnp.sum(y * y, axis=-1, keepdims=True)
            xy = jnp.sum(x * y, axis=-1, keepdims=True)
            num = (1.0 + 2.0 * c * xy + c * y2) * x + (1.0 - c * x2) * y
            den = 1.0 + 2.0 * c * xy + c * c * x2 * y2
            return num / jnp.clip(den, MIN_NORM)
        N, E, R, D = (6250, 50000, 230, 16)
        key = jax.random.key(seed)
        ks = jax.random.split(key, 8)
        h_hyper = project_to_ball(0.1 * jax.random.normal(ks[0], (N, D), dtype=jnp.float32), C)
        node_norm = jax.random.uniform(ks[1], (N, 1), dtype=jnp.float32)
        xav = float(np.sqrt(2.0 / (D + D)))
        rel_weight = xav * jax.random.normal(ks[2], (R, D, D), dtype=jnp.float32)
        loop_weight = xav * jax.random.normal(ks[3], (D, D), dtype=jnp.float32)
        rel_emb = 0.1 * jax.random.normal(ks[4], (R, D), dtype=jnp.float32)
        src = jax.random.randint(ks[5], (E,), 0, N, dtype=jnp.int32)
        dst = jax.random.randint(ks[6], (E,), 0, N, dtype=jnp.int32)
        etype = jax.random.randint(ks[7], (E,), 0, R, dtype=jnp.int32)
        return {'h_hyper': h_hyper, 'node_norm': node_norm, 'rel_weight': rel_weight, 'loop_weight': loop_weight, 'rel_emb': rel_emb, 'src': src, 'dst': dst, 'etype': etype}
    _L0_gnn_all = _L0_gnn_setup()
    _L0_gnn_in = {k: v for k, v in _L0_gnn_all.items() if k in ('rel_weight', 'loop_weight', 'rel_emb')}
    del _L0_gnn_all

    def _L1_gnn_setup():
        import jax, jax.numpy as jnp
        import numpy as np
        N_NODES = 12500
        N_EDGES = 400000
        D_NODE = 16
        D_EDGE = 8
        D_HIDDEN = 16
        key = jax.random.key(seed)
        ks = jax.random.split(key, 8)
        node_features = jax.random.normal(ks[0], (N_NODES, D_NODE), dtype=jnp.float32)
        edge_attr_e3nn = jax.random.normal(ks[1], (N_EDGES, D_EDGE), dtype=jnp.float32)
        node_attr_scalar_raw = jax.random.normal(ks[2], (N_NODES, 1), dtype=jnp.float32)
        W_msg_tp = jax.random.normal(ks[3], (D_NODE, D_EDGE, D_HIDDEN), dtype=jnp.float32)
        W_msg_lin = jax.random.normal(ks[4], (D_HIDDEN, D_HIDDEN), dtype=jnp.float32)
        W_upd_tp = jax.random.normal(ks[5], (D_NODE, D_HIDDEN, D_HIDDEN), dtype=jnp.float32)
        W_upd_lin = jax.random.normal(ks[6], (D_HIDDEN, D_NODE), dtype=jnp.float32)
        edge_index = jax.random.randint(ks[7], (2, N_EDGES), 0, N_NODES, dtype=jnp.int64)
        return {'node_features': node_features, 'edge_attr_e3nn': edge_attr_e3nn, 'node_attr_scalar_raw': node_attr_scalar_raw, 'W_msg_tp': W_msg_tp, 'W_msg_lin': W_msg_lin, 'W_upd_tp': W_upd_tp, 'W_upd_lin': W_upd_lin, 'edge_index': edge_index}
    _L1_gnn_all = _L1_gnn_setup()
    _L1_gnn_in = {k: v for k, v in _L1_gnn_all.items() if k in ('W_msg_tp', 'W_msg_lin', 'W_upd_tp', 'W_upd_lin')}
    del _L1_gnn_all

    def _L2_gnn_setup():
        import jax, jax.numpy as jnp
        import numpy as np
        N = 62500
        E = 1000000
        C = 16

        def gcn_conv(x, edge_index, W):
            n = x.shape[0]
            h = x @ W
            loops = jnp.arange(n, dtype=edge_index.dtype)
            src = jnp.concatenate([edge_index[0], loops])
            dst = jnp.concatenate([edge_index[1], loops])
            deg = jax.ops.segment_sum(jnp.ones_like(dst, dtype=h.dtype), dst, num_segments=n)
            dinv = jnp.where(deg > 0, jax.lax.rsqrt(deg), 0.0)
            norm = dinv[src] * dinv[dst]
            msg = h[src] * norm[:, None]
            return jax.ops.segment_sum(msg, dst, num_segments=n)
        key = jax.random.key(seed)
        ks = jax.random.split(key, 8)
        xx = jax.random.normal(ks[0], (N, C), dtype=jnp.float32)
        edge_index = jax.random.randint(ks[1], (2, E), 0, N, dtype=jnp.int64)
        W_gcn = jax.random.normal(ks[2], (C, 3 * C), dtype=jnp.float32) / np.sqrt(C)
        W1 = jax.random.normal(ks[3], (3 * C, 32), dtype=jnp.float32) / np.sqrt(3 * C)
        b1 = jnp.zeros((32,), dtype=jnp.float32)
        W2 = jax.random.normal(ks[4], (32, C), dtype=jnp.float32) / np.sqrt(32)
        b2 = jnp.zeros((C,), dtype=jnp.float32)
        return {'xx': xx, 'edge_index': edge_index, 'W_gcn': W_gcn, 'W1': W1, 'b1': b1, 'W2': W2, 'b2': b2}
    _L2_gnn_all = _L2_gnn_setup()
    _L2_gnn_in = {k: v for k, v in _L2_gnn_all.items() if k in ('W_gcn', 'W1', 'b1', 'W2', 'b2')}
    del _L2_gnn_all

    def _L3_gnn_setup():
        import jax, jax.numpy as jnp
        import numpy as np
        N_NODES = 12500
        N_EDGES = 62500
        IND = 16
        OUT = 16
        EDGE_DIM = 16
        HID = IND * OUT
        BN_EPS = 1e-05
        key = jax.random.key(seed)
        ks = jax.random.split(key, 12)
        x = jax.random.normal(ks[0], (N_NODES, IND), dtype=jnp.float32)
        edge_index = jax.random.randint(ks[1], (2, N_EDGES), 0, N_NODES, dtype=jnp.int64)
        edge_attr = jax.random.normal(ks[2], (N_EDGES, EDGE_DIM), dtype=jnp.float32)
        W1 = jax.random.normal(ks[3], (EDGE_DIM, HID), dtype=jnp.float32) * (1.0 / np.sqrt(EDGE_DIM))
        b1 = jnp.zeros((HID,), dtype=jnp.float32)
        W2 = jax.random.normal(ks[4], (HID, HID), dtype=jnp.float32) * (1.0 / np.sqrt(HID))
        b2 = jnp.zeros((HID,), dtype=jnp.float32)
        root = jax.random.normal(ks[5], (IND, OUT), dtype=jnp.float32) * (1.0 / np.sqrt(IND))
        bias = jnp.zeros((OUT,), dtype=jnp.float32)
        gamma = jnp.ones((OUT,), dtype=jnp.float32)
        beta = jnp.zeros((OUT,), dtype=jnp.float32)
        return {'x': x, 'edge_index': edge_index, 'edge_attr': edge_attr, 'W1': W1, 'b1': b1, 'W2': W2, 'b2': b2, 'root': root, 'bias': bias, 'gamma': gamma, 'beta': beta}
    _L3_gnn_all = _L3_gnn_setup()
    _L3_gnn_in = {k: v for k, v in _L3_gnn_all.items() if k in ('W1', 'b1', 'W2', 'b2', 'root', 'bias', 'gamma', 'beta')}
    del _L3_gnn_all
    return {'x': x, 'src': src, 'dst': dst, 'edge_attr_16': edge_attr_16, 'edge_attr_8': edge_attr_8, 'edge_type_230': edge_type_230, 'node_vec1': node_vec1, 'L0_gnn_rel_weight': _L0_gnn_in['rel_weight'], 'L0_gnn_loop_weight': _L0_gnn_in['loop_weight'], 'L0_gnn_rel_emb': _L0_gnn_in['rel_emb'], 'L1_gnn_W_msg_tp': _L1_gnn_in['W_msg_tp'], 'L1_gnn_W_msg_lin': _L1_gnn_in['W_msg_lin'], 'L1_gnn_W_upd_tp': _L1_gnn_in['W_upd_tp'], 'L1_gnn_W_upd_lin': _L1_gnn_in['W_upd_lin'], 'L2_gnn_W_gcn': _L2_gnn_in['W_gcn'], 'L2_gnn_W1': _L2_gnn_in['W1'], 'L2_gnn_b1': _L2_gnn_in['b1'], 'L2_gnn_W2': _L2_gnn_in['W2'], 'L2_gnn_b2': _L2_gnn_in['b2'], 'L3_gnn_W1': _L3_gnn_in['W1'], 'L3_gnn_b1': _L3_gnn_in['b1'], 'L3_gnn_W2': _L3_gnn_in['W2'], 'L3_gnn_b2': _L3_gnn_in['b2'], 'L3_gnn_root': _L3_gnn_in['root'], 'L3_gnn_bias': _L3_gnn_in['bias'], 'L3_gnn_gamma': _L3_gnn_in['gamma'], 'L3_gnn_beta': _L3_gnn_in['beta']}

def reference(x, src, dst, edge_attr_16, edge_attr_8, edge_type_230, node_vec1, L0_gnn_rel_weight, L0_gnn_loop_weight, L0_gnn_rel_emb, L1_gnn_W_msg_tp, L1_gnn_W_msg_lin, L1_gnn_W_upd_tp, L1_gnn_W_upd_lin, L2_gnn_W_gcn, L2_gnn_W1, L2_gnn_b1, L2_gnn_W2, L2_gnn_b2, L3_gnn_W1, L3_gnn_b1, L3_gnn_W2, L3_gnn_b2, L3_gnn_root, L3_gnn_bias, L3_gnn_gamma, L3_gnn_beta):
    import jax
    import jax.numpy as jnp

    def _L0_gnn_ref(h_hyper, node_norm, rel_weight, loop_weight, rel_emb, src, dst, etype):
        import jax, jax.numpy as jnp
        import numpy as np
        C = 0.01
        EPS = 1e-06
        MIN_NORM = 1e-10
        BALL_EPS = 1e-05

        def _norm(x):
            return jnp.sqrt(jnp.clip(jnp.sum(x * x, axis=-1, keepdims=True), MIN_NORM))

        def log_map_zero(x, c):
            sc = jnp.sqrt(c)
            n = _norm(x)
            return jnp.arctanh(jnp.clip(sc * n, -1.0 + BALL_EPS, 1.0 - BALL_EPS)) * x / (sc * n)

        def exp_map_zero(v, c):
            sc = jnp.sqrt(c)
            n = _norm(v)
            return jnp.tanh(sc * n) * v / (sc * n)

        def project_to_ball(x, c):
            n = _norm(x)
            maxn = (1.0 - BALL_EPS) / jnp.sqrt(c)
            return jnp.where(n > maxn, x * (maxn / n), x)

        def mobius_add(x, y, c):
            x2 = jnp.sum(x * x, axis=-1, keepdims=True)
            y2 = jnp.sum(y * y, axis=-1, keepdims=True)
            xy = jnp.sum(x * y, axis=-1, keepdims=True)
            num = (1.0 + 2.0 * c * xy + c * y2) * x + (1.0 - c * x2) * y
            den = 1.0 + 2.0 * c * xy + c * c * x2 * y2
            return num / jnp.clip(den, MIN_NORM)
        c = C
        N = h_hyper.shape[0]
        h_tan = log_map_zero(h_hyper, c)
        msg_tan = jnp.einsum('ei,eio->eo', h_tan[src], rel_weight[etype])
        msg_tan = msg_tan + rel_emb[etype]
        msg = exp_map_zero(msg_tan, c)
        en = node_norm[dst, 0]
        norm_sum = jax.ops.segment_sum(en, dst, num_segments=N)
        w = en / (norm_sum[dst] + EPS)
        lam = 2.0 / (1.0 - c * jnp.sum(msg * msg, axis=-1) + EPS)
        wl = w * lam
        numer = jax.ops.segment_sum(wl[:, None] * msg, dst, num_segments=N)
        denom = jax.ops.segment_sum(wl, dst, num_segments=N) + EPS
        h_agg = project_to_ball(numer / denom[:, None], c)
        loop_hyp = exp_map_zero(h_tan @ loop_weight, c)
        h_new = mobius_add(h_agg, loop_hyp, c)
        return h_new

    def _L1_gnn_ref(node_features, edge_attr_e3nn, node_attr_scalar_raw, W_msg_tp, W_msg_lin, W_upd_tp, W_upd_lin, edge_index):
        import jax, jax.numpy as jnp
        import numpy as np
        N_NODES = 12500
        N_EDGES = 400000
        D_NODE = 16
        D_EDGE = 8
        D_HIDDEN = 16
        n_nodes = node_features.shape[0]
        row = edge_index[0]
        col = edge_index[1]
        norm_msg_tp = 1.0 / np.float32(np.sqrt(D_NODE * D_EDGE))
        norm_upd_tp = 1.0 / np.float32(np.sqrt(D_NODE * D_HIDDEN))
        norm_lin = 1.0 / np.float32(np.sqrt(D_HIDDEN))
        x_j = node_features[col]
        m = jnp.einsum('ei,ej,ijh->eh', x_j, edge_attr_e3nn, W_msg_tp) * norm_msg_tp
        m = jax.nn.silu(m)
        m = m @ W_msg_lin * norm_lin
        agg = jax.ops.segment_sum(m, row, num_segments=n_nodes)
        u = jnp.einsum('ni,nh,ihk->nk', node_features, agg, W_upd_tp) * norm_upd_tp
        u = jax.nn.silu(u)
        u = u @ W_upd_lin * norm_lin
        return node_features + u

    def _L2_gnn_ref(xx, edge_index, W_gcn, W1, b1, W2, b2):
        import jax, jax.numpy as jnp
        import numpy as np
        N = 62500
        E = 1000000
        C = 16

        def gcn_conv(x, edge_index, W):
            n = x.shape[0]
            h = x @ W
            loops = jnp.arange(n, dtype=edge_index.dtype)
            src = jnp.concatenate([edge_index[0], loops])
            dst = jnp.concatenate([edge_index[1], loops])
            deg = jax.ops.segment_sum(jnp.ones_like(dst, dtype=h.dtype), dst, num_segments=n)
            dinv = jnp.where(deg > 0, jax.lax.rsqrt(deg), 0.0)
            norm = dinv[src] * dinv[dst]
            msg = h[src] * norm[:, None]
            return jax.ops.segment_sum(msg, dst, num_segments=n)
        features = gcn_conv(xx, edge_index, W_gcn)
        update = jax.nn.relu(features @ W1 + b1) @ W2 + b2
        return xx + update

    def _L3_gnn_ref(x, edge_index, edge_attr, W1, b1, W2, b2, root, bias, gamma, beta):
        import jax, jax.numpy as jnp
        import numpy as np
        N_NODES = 12500
        N_EDGES = 62500
        IND = 16
        OUT = 16
        EDGE_DIM = 16
        HID = IND * OUT
        BN_EPS = 1e-05
        n_nodes, ind = x.shape
        out_dim = root.shape[1]
        src, dst = (edge_index[0], edge_index[1])
        h = jax.nn.relu(edge_attr @ W1 + b1)
        w_edge = (h @ W2 + b2).reshape(-1, ind, out_dim)
        msgs = jnp.einsum('ei,eio->eo', x[src], w_edge)
        aggr = jax.ops.segment_sum(msgs, dst, num_segments=n_nodes)
        out = aggr + x @ root + bias
        mean = out.mean(axis=0)
        var = out.var(axis=0)
        out = (out - mean) / jnp.sqrt(var + BN_EPS) * gamma + beta
        return jax.nn.relu(out)
    edge_index = jnp.stack([src, dst])
    deg = jnp.maximum(jax.ops.segment_sum(jnp.ones(dst.shape, jnp.float32), dst, num_segments=12500), 1.0)
    deg_isqrt = deg ** (-0.5)
    h = jnp.maximum(_layernorm(x, axis=-1), 0.0)
    x = x + _L0_gnn_ref(h, deg_isqrt[:, None], L0_gnn_rel_weight, L0_gnn_loop_weight, L0_gnn_rel_emb, src, dst, edge_type_230)
    h = jnp.maximum(_layernorm(x, axis=-1), 0.0)
    x = x + _L1_gnn_ref(h, edge_attr_8, node_vec1, L1_gnn_W_msg_tp, L1_gnn_W_msg_lin, L1_gnn_W_upd_tp, L1_gnn_W_upd_lin, edge_index)
    h = jnp.maximum(_layernorm(x, axis=-1), 0.0)
    x = x + _L2_gnn_ref(h, edge_index, L2_gnn_W_gcn, L2_gnn_W1, L2_gnn_b1, L2_gnn_W2, L2_gnn_b2)
    h = jnp.maximum(_layernorm(x, axis=-1), 0.0)
    x = x + _L3_gnn_ref(h, edge_index, edge_attr_16, L3_gnn_W1, L3_gnn_b1, L3_gnn_W2, L3_gnn_b2, L3_gnn_root, L3_gnn_bias, L3_gnn_gamma, L3_gnn_beta)
    return x

_drawn_inputs = setup_inputs


def setup_inputs(seed=0):
    import zlib

    import numpy as np

    out = dict(_drawn_inputs(seed))
    spreads = {'L2_gnn_b1': (0.0, 0.8),
     'L2_gnn_b2': (0.0, 0.302),
     'L3_gnn_b1': (0.0, 0.339),
     'L3_gnn_b2': (0.0, 0.1),
     'L3_gnn_bias': (0.0, 0.8),
     'L3_gnn_gamma': (1.0, 0.2),
     'L3_gnn_beta': (0.0, 0.601)}
    factors = {'L3_gnn_root': 8.0}
    for name, (base, spread) in spreads.items():
        noise = np.random.default_rng([zlib.crc32(name.encode()), seed]).standard_normal(out[name].shape)
        drawn = base * np.exp(spread * noise) if base else spread * noise
        out[name] = jnp.asarray(drawn.astype(out[name].dtype))
    for name, factor in factors.items():
        out[name] = (out[name] * factor).astype(out[name].dtype)
    return out
```

```python
from contextlib import ExitStack

import concourse.bass as bass
from concourse import mybir

ALU = mybir.AluOpType
ACT = mybir.ActivationFunctionType
AX = mybir.AxisListType
F32 = mybir.dt.float32
I32 = mybir.dt.int32
MAX = bass.bass_isa.ReduceOp.max
ds = bass.ds

P = 128
N = 12500
E = 400000
D = 16
R = 230
DE = 8
NB = -(-N // P)
NP = NB * P
GB = 7
NG = NB // GB
G = 5
SUP = E // (P * G)
S = 5
TC = S * G
CH = SUP // S
PAIRS = CH // 2
WIN = 128
ACCN = NP + P
VW = 32
K_T = D + 1
TROW = R * D
PIECE = 2 * 368
NPIECE = TROW // PIECE
C = 0.01
SQC = 0.1
EPS = 1e-6
MIN_NORM = 1e-10
BALL_EPS = 1e-5
LN_EPS = 1e-5
NORM_MSG = 1.0 / float((D * DE) ** 0.5)
NORM_UPD = 1.0 / D
NORM_LIN = 0.25
FAST, GENERAL = "sorted", "general"
YW = D * DE
ATANH_TERMS = 10
WEIGHT_DMAS = 2 + 5 * GB + 2 * GB + 4 + 2 + 5 + 2 * G + 1
SEQS = [("loop", NG, GB * D, 2), ("table1", NG, GB * YW, 2), ("msg_lin", NG, GB * D, 2), ("update", NG, GB * 256, 1),
        ("upd_lin", NG, GB * D, 2), ("gcn1", NG, GB * 32, 2), ("gcn2", -(-NB // 4), 4 * D, 2),
        ("bias_w", NG, GB * D, 2), ("root", NG, GB * D, 2)]
SEQ_GROUPS = {n: g for n, g, _, _ in SEQS}
SEQ_COLS = {n: c for n, _, c, _ in SEQS}
SEQ_SLOTS = {n: s for n, _, _, s in SEQS}
SEQ = {n: sum(g for _, g, _, _ in SEQS[:i]) for i, (n, _, _, _) in enumerate(SEQS)}


def gnn_kernel(nc, t, out):
    ctx = ExitStack()
    with ctx:
        def sb(name, shape, dt=F32):
            return ctx.enter_context(nc.sbuf_tensor(name, shape, dt))

        def sem(name):
            return ctx.enter_context(nc.semaphore(name))

        def flat(a):
            return a.rearrange("p b w -> p (b w)")

        msg_tab = nc.dram_tensor("message_table", [NP * R, D], F32)
        y_tab = nc.dram_tensor("layer1_table", [NP + WIN, YW], F32)
        z_tab = nc.dram_tensor("layer2_table", [NP, D], F32)
        h_tab = nc.dram_tensor("layer3_table", [NP, D], F32)
        wc_dram = nc.dram_tensor("layer2_weight", [D, 32], F32)
        acc16 = [nc.dram_tensor(f"acc16_{g}", [ACCN, D], F32) for g in range(G)]
        acc32 = [nc.dram_tensor(f"acc32_{g}", [ACCN, VW], F32) for g in range(G)]

        x = sb("x", [P, NB, D])
        h = sb("h", [P, NB, D])
        src = sb("src", [P, SUP, G], I32)
        dst = sb("dst", [P, SUP, G], I32)
        tix = sb("tix", [P, SUP, G], I32)
        rel = sb("rel", [P, SUP, G])
        base_i = sb("base_i", [P, SUP + 3], I32)
        base_p = sb("base_p", [P, SUP])
        accT = sb("accT", [P, ACCN])
        agg = sb("agg", [P, NB, VW])
        htan = sb("htan", [P, NB, D])
        ident = sb("ident", [P, P])
        first_row = sb("first_row", [P, P])
        ones = sb("ones", [P, P])
        lower = sb("lower", [P, P])
        iota_i = sb("iota_i", [P, WIN], I32)
        iota = sb("iota", [P, WIN])
        part_i = sb("part_i", [P, 1], I32)
        part = sb("part", [P, 1])
        junk = sb("junk", [P, 1])
        mask_i = sb("mask_i", [P, NB], I32)
        mask = sb("mask", [P, NB])
        range_in = sb("range_in", [P, 2])
        range_all = sb("range_all", [P, 2])
        fits = sb("fits", [P, 2])
        flag = sb("flag", [P, 1], I32)
        deg = sb("deg", [P, NB])
        wt_space = sb("wt_space", [P, TROW])
        wt = wt_space[0:K_T, :].rearrange("k (r o) -> k r o", o=D)
        wbd = sb("wbd", [P, 5, GB * D])
        ybd = sb("ybd", [P, GB * YW])
        ubd = sb("ubd", [P, GB * 256])
        cbd = sb("cbd", [P, GB * 32])
        w2bd = sb("w2bd", [P, 4 * D])
        wgT = sb("wgT", [48, D])
        w1g = sb("w1g", [48, 32])
        wc = sb("wc", [D, 32])
        b1g = sb("b1g", [P, 32])
        b2g = sb("b2g", [P, D])
        bias3 = sb("bias3", [P, D])
        gamma3 = sb("gamma3", [P, D])
        beta3 = sb("beta3", [P, D])
        w1x = sb("w1x", [G * D + 1, G, 256])
        w2x = sb("w2x", [P, 2, 256])
        nv = [sb(f"nv{i}", [P, NB]) for i in range(6)]
        big = sb("big", [P, NB, D])
        xt = sb("xt", [P, 2, P])
        gout = sb("gout", [P, GB * 256])
        bn = sb("bn", [P, 8, D])
        ibuf = sb("ibuf", [P, 2, TC], I32)
        rows = sb("rows", [P, 2, TC, D])
        cnt = sb("cnt", [P, G])
        keyd = sb("keyd", [P, G])
        idx2 = sb("idx2", [P, 2, G], I32)
        summed = sb("summed", [P, 2, G, VW])
        summed16 = sb("summed16", [P, 2, G, D])
        sv = [sb(f"sv{i}", [P, TC]) for i in range(8)]
        mpre = sb("mpre", [P, 2, G, D])
        mval = sb("mval", [P, 2, G, D])
        agg_space = flat(agg[:, :, :])
        work = agg_space[:, 0:G * 256]
        vals = agg_space[:, G * 256:G * 256 + 2 * TC * VW].rearrange("p (a t w) -> p a t w", a=2, t=TC)
        onehot = gout[:, 0:2 * G * WIN].rearrange("p (a g n) -> p a g n", a=2, g=G)
        same = wt_space[:, 0:2 * G * P].rearrange("p (a g n) -> p a g n", a=2, g=G)
        keys = wt_space[:, 2 * G * P:4 * G * P].bitcast(I32).rearrange("p (a n) -> p a n", a=2)
        eaT = wt_space[0:G * D + 1, 4 * G * P:4 * G * P + 2 * P].rearrange("p (a n) -> p a n", a=2)
        hid = wt_space[:, 4 * G * P + 2 * P:4 * G * P + 6 * P].rearrange("p (a n) -> p a n", a=2)
        tix_space = flat(tix[:, :, :])
        tix_f = tix_space.bitcast(F32)
        drow = tix_space[:, 0:2 * G * P].rearrange("p (a n) -> p a n", a=2)
        o1 = 2 * G * P
        ea8 = tix_f[:, o1:o1 + 2 * TC * DE].rearrange("p (a t w) -> p a t w", a=2, t=TC)
        o2 = o1 + 2 * TC * DE
        ywin = tix_f[:, o2:o2 + 2 * YW].rearrange("p (a n) -> p a n", a=2)
        o3 = o2 + 2 * YW
        ea = tix_f[:, o3:o3 + 2 * S * (G * D + 1)].rearrange("p (a s w) -> p a s w", a=2, s=S)
        stg = sb("stg", [P, 2, K_T])
        lt = sb("lt", [K_T, 2, P])
        tbuf = accT[:, 0:2 * TROW].rearrange("p (a n) -> p a n", a=2)
        yrow = accT[:, 0:2 * G * YW].rearrange("p (a g w) -> p a g w", a=2, g=G)

        ps = ctx.enter_context(nc.psum_tensor("ps", [P, 8, 512], F32))
        psf = ps[:, :, :].rearrange("p b n -> p (b n)")

        cleared, consts, x_in, weights_in, idx_in, iota_done = (
            sem("cleared"), sem("consts"), sem("x_in"), sem("weights_in"), sem("idx_in"), sem("iota_done"))
        base_asked, base_done = sem("base_asked"), sem("base_done")
        range_ready, range_reduced, flag_ready = sem("range_ready"), sem("range_reduced"), sem("flag_ready")
        fn_asked, fn_done = sem("fn_asked"), sem("fn_done")
        seq_ready, turned, turn_copied, product_done, product_used = (
            sem("seq_ready"), sem("turned"), sem("turn_copied"), sem("product_done"), sem("product_used"))
        t_staged, t_turned, t_lhs, t_prod, t_evA, t_evD = (
            sem("t_staged"), sem("t_turned"), sem("t_lhs"), sem("t_prod"), sem("t_evA"), sem("t_evD"))
        t_stored = [sem("t_stored0"), sem("t_stored1")]
        acc_cleared = sem("acc_cleared")
        table_ready, table_stored = sem("table_ready"), sem("table_stored")
        y_stored = [sem("y_stored0"), sem("y_stored1")]
        wc_done, wc_copied, wc_stored, cbd_in = sem("wc_done"), sem("wc_copied"), sem("wc_stored"), sem("cbd_in")
        bn_asked, bn_done = sem("bn_asked"), sem("bn_done")
        out_ready, out_stored = sem("out_ready"), sem("out_stored")
        pool_turn = sem("pool_turn")

        loop_sems = {}

        class Loop:

            def __init__(self, layer, mode):
                self.layer, self.mode = layer, mode
                self.window = layer != 1 and mode == FAST
                self.dedupe = not self.window
                self.pick = layer == 1 and mode == FAST
                self.gathers = not self.pick
                self.width = D if layer == 1 else VW
                self.acc = acc16 if layer == 1 else acc32
                self.key = src if layer == 1 else dst
                self.key_dram = t["src"] if layer == 1 else t["dst"]
                self.idx = {0: tix, 1: dst, 2: src, 3: src}[layer]
                self.table = {0: msg_tab, 1: y_tab, 2: z_tab, 3: h_tab}[layer]

                def s(name):
                    name = f"L{layer}_{name}"
                    if name not in loop_sems:
                        loop_sems[name] = sem(name)
                    return loop_sems[name]

                if self.gathers:
                    self.idx_staged = s("idx_staged")
                    self.gathered = [s("gathered0"), s("gathered1")]
                    self.rows_free = s("rows_free")
                self.vals_ready = s("vals_ready")
                if self.window:
                    self.matrix_ready, self.sums_done, self.sums_taken = (
                        s("matrix_ready"), s("sums_done"), s("sums_taken"))
                    self.loop_done, self.agg_done = s("loop_done"), s("agg_done")
                else:
                    self.keys_in = [s("keys_in0"), s("keys_in1")]
                    self.keys_free, self.matrix_ready, self.sums_done, self.sums_taken = (
                        s("keys_free"), s("matrix_ready"), s("sums_done"), s("sums_taken"))
                    self.idx2_ready, self.slot_done = s("idx2_ready"), s("slot_done")
                    self.scattered = [s(f"scattered{g}") for g in range(G)]
                    self.acc_zeroed, self.loop_done, self.acc_loaded, self.agg_done = (
                        s("acc_zeroed"), s("loop_done"), s("acc_loaded"), s("agg_done"))
                if layer == 0:
                    self.norm_asked, self.norm_done = s("norm_asked"), s("norm_done")
                if layer in (1, 3):
                    self.ea_in = [s("ea_in0"), s("ea_in1")]
                if layer == 1:
                    self.ea_free, self.m_ready = s("ea_free"), s("m_ready")
                if self.pick:
                    self.pick_ready, self.picked = s("pick_ready"), s("picked")
                    self.ywin_in = [s("ywin_in0"), s("ywin_in1")]
                if layer == 3:
                    self.ea_turned, self.ea_copied, self.hid_done, self.relu_done, self.w_done, self.w_used = (
                        s("ea_turned"), s("ea_copied"), s("hid_done"), s("relu_done"), s("w_done"), s("w_used"))

        loops = {(l, m): Loop(l, m) for l in range(4) for m in (FAST, GENERAL)}

        def by_tile(a):
            return a.rearrange("(s p g) -> p s g", p=P, g=G)

        def by_tile_rows(a):
            return a.rearrange("(s p g) w -> p s (g w)", p=P, g=G)

        def node_rows(a):
            return a[0:NP, :].rearrange("(p b) w -> p (b w)", p=P)

        def run_chunks(eng, body, peel=False):
            if peel:
                body(0, 0, False)
                body(0, 1, False)
            with eng.Fori(int(peel), PAIRS) as k:
                body(k, 0, False)
                body(k, 1, False)
            body(PAIRS, 0, True)

        def either(eng, layer, fn):
            fit = eng.value_load(flag[0:1, 0:1], min_val=0, max_val=1)
            with eng.If(fit > 0):
                fn(loops[layer, FAST])
            with eng.Else():
                fn(loops[layer, GENERAL])

        def slot_of(par, j):
            return (S * par + j) % 2

        def slot_count(k, par, j):
            return S * k + (S * par + j) // 2 + 1

        def table_piece(par, i):
            q = 2 * ((NPIECE * par + i) % 2)
            return ps[:, q:q + 2, 0:PIECE // 2]

        def group_out(name, g):
            n, slots = SEQ_COLS[name], SEQ_SLOTS[name]
            first = 2 * (g % slots)
            banks = max(1, n // 448)
            if banks == 1:
                return ps[:, first, 0:n]
            return ps[:, first:first + banks, 0:448]

        def turn_out(g, cols):
            return ps[0:cols, 6 + g % 2, 0:P]

        block = ctx.enter_context(nc.Block())

        @block.sync
        def _(sp):
            full = (N // NB) * NB
            last = N // NB
            flat_x = t["x"].rearrange("n d -> (n d)")
            sp.wait_ge(cleared, 1)
            sp.dma_start(flat(x[0:last, :, :]), t["x"][0:full, :].rearrange("(p b) d -> p (b d)", b=NB)).then_inc(x_in, 16)
            sp.dma_start(flat(x[last:last + 1, 0:N - full, :]),
                         flat_x[full * D:N * D].rearrange("(a n) -> a n", a=1)).then_inc(x_in, 16)
            for tile, name in ((dst, "dst"), (src, "src"), (tix, "edge_type_230")):
                sp.dma_start(tile[:, :, :], by_tile(t[name])).then_inc(idx_in, 16)
            sp.dma_start(wt[0:D, :, :], t["L0_gnn_rel_weight"].rearrange("r i o -> i r o")).then_inc(weights_in, 16)
            sp.dma_start(wt[D:D + 1, :, :], t["L0_gnn_rel_emb"].rearrange("(a r) o -> a r o", a=1)).then_inc(weights_in, 16)

            for s in t_stored:
                sp.sem_inc(s, 16)
            tdram = msg_tab[:, :].rearrange("(p b r) w -> p b (r w)", p=P, b=NB)
            with sp.Fori(0, NB // 2) as k:
                for par in range(2):
                    b = 2 * k + par
                    sp.wait_ge(t_evA, 3 * b + 4)
                    sp.wait_ge(t_evD, 2 * b + 3)
                    sp.dma_start(tdram[:, ds(b, 1), :], tbuf[:, par:par + 1, :]).then_inc(t_stored[par], 16)

            def edges(L):
                if L.dedupe:
                    sp.wait_ge(acc_cleared, L.layer + 1)
                    for g in range(G):
                        sp.dma_start(L.acc[g][:, :].rearrange("(p n) w -> p (n w)", p=P),
                                     accT[:, 0:ACCN // P * L.width]).then_inc(L.acc_zeroed, 16)

                def body(k, par, last):
                    c = 2 * k + par
                    if L.layer == 1:
                        sp.wait_ge(L.ea_free, c + 1)
                        sp.dma_start(ea8[:, par, :, :].rearrange("p (s g) w -> p s (g w)", g=G),
                                     by_tile_rows(t["edge_attr_8"])[:, ds(S * c, S), :]).then_inc(L.ea_in[par], 16)
                    if L.layer == 3:
                        sp.wait_ge(L.rows_free, c + 1)
                        sp.dma_start(ea[:, par, :, 0:G * D],
                                     by_tile_rows(t["edge_attr_16"])[:, ds(S * c, S), :]).then_inc(L.ea_in[par], 16)
                    if not L.dedupe:
                        return
                    if L.pick:
                        _, bases = nc.values_load_multi_w_load_instructions(
                            base_i[0:1, ds(S * c, S)], engines=[sp.engine], min_val=0, max_val=NP)
                    for j in range(S):
                        s, slot = S * c + j, slot_of(par, j)
                        sp.wait_ge(L.keys_free, s + 1)
                        sp.dma_start(keys[:, slot, :], L.key_dram[ds(s * P * G, P * G)].partition_broadcast(P))\
                          .then_inc(L.keys_in[slot], 16)
                        if L.pick:
                            sp.dma_start(drow[:, slot, :], t["dst"][ds(s * P * G, P * G)].partition_broadcast(P))\
                              .then_inc(L.keys_in[slot], 16)
                            sp.wait_ge(L.picked, s + 1)
                            sp.dma_start(ywin[:, slot, :], y_tab[ds(bases[j], WIN), :]).then_inc(L.ywin_in[slot], 16)

                if L.dedupe or L.layer == 3:
                    run_chunks(sp, body)
                if L.dedupe:
                    w = L.width * NB
                    sp.wait_ge(L.loop_done, 1)
                    for g in range(4):
                        sp.dma_start(accT[:, g * w:(g + 1) * w], node_rows(L.acc[g])).then_inc(L.acc_loaded, 16)
                    sp.wait_ge(L.agg_done, 1)
                    sp.dma_start(accT[:, 0:w], node_rows(L.acc[4])).then_inc(L.acc_loaded, 16)

            sp.wait_ge(flag_ready, 1)
            either(sp, 0, edges)
            for g in range(NG):
                sp.wait_ge(product_used, SEQ["table1"] + g + 1)
                sp.dma_start(node_rows(y_tab)[:, g * GB * YW:(g + 1) * GB * YW],
                             gout[:, (g % 2) * GB * YW:(g % 2 + 1) * GB * YW]).then_inc(y_stored[g % 2], 16)
            sp.dma_start(y_tab[NP:NP + WIN, :], ones[:, :]).then_inc(table_stored, 16)
            for s in y_stored:
                sp.wait_ge(s, 16 * (NG // 2))
            sp.wait_ge(table_stored, 16)
            either(sp, 1, edges)
            sp.wait_ge(table_ready, 1)
            sp.dma_start(node_rows(z_tab), flat(big[:, :, :])).then_inc(table_stored, 16)
            either(sp, 2, edges)
            sp.wait_ge(table_ready, 2)
            sp.dma_start(node_rows(h_tab), flat(h[:, :, :])).then_inc(table_stored, 16)
            either(sp, 3, edges)
            sp.wait_ge(out_ready, 1)
            sp.dma_start(out[0:full, :].rearrange("(p b) d -> p (b d)", b=NB), flat(x[0:last, :, :])).then_inc(out_stored, 16)
            sp.dma_start(out.rearrange("n d -> (n d)")[full * D:N * D].rearrange("(a n) -> a n", a=1),
                         flat(x[last:last + 1, 0:N - full, :])).then_inc(out_stored, 16)
            sp.wait_ge(out_stored, 32)

        @block.gpsimd
        def _(pool):
            pool.iota(iota_i[:, :], pattern=[[1, WIN]], base=0, channel_multiplier=0).then_inc(iota_done, 1)
            pool.iota(part_i[:, :], pattern=[[0, 1]], base=0, channel_multiplier=1).then_inc(iota_done, 1)
            pool.iota(mask_i[:, :], pattern=[[1, NB]], base=0, channel_multiplier=NB).then_inc(iota_done, 1)
            pool.memset(ident[:, :], 0.0)
            pool.memset(ones[:, :], 1.0)
            pool.drain()
            pool.affine_select(out=ident[:, :], in_=ident[:, :], compare_op=ALU.not_equal, fill=1.0,
                               base=0, pattern=[[-1, P]], channel_multiplier=1)
            pool.affine_select(out=lower[:, :], in_=ones[:, :], compare_op=ALU.is_gt, fill=0.0,
                               base=0, pattern=[[-1, P]], channel_multiplier=1)
            pool.affine_select(out=first_row[:, :], in_=ones[:, :], compare_op=ALU.is_equal, fill=0.0,
                               base=0, pattern=[[0, P]], channel_multiplier=1)
            pool.drain()
            pool.sem_inc(consts, 1)
            pool.wait_ge(range_ready, 1)
            pool.partition_all_reduce(range_all[:, :], range_in[:, :], P, MAX).then_inc(range_reduced, 1)

            def before_dma():
                pool.sem_inc(pool_turn, 1)

            def edges(L):
                def gather(k, par):
                    c = 2 * k + par
                    pool.wait_ge(L.idx_staged, c + 1)
                    pool.wait_ge(L.rows_free, c + 1)
                    before_dma()
                    for i in range(TC):
                        pool.indirect_dma_start(rows[:, par, i, :], None, L.table[:, :],
                                                bass.IndirectOffsetOnAxis(ap=ibuf[:, par, i:i + 1], axis=0))\
                            .then_inc(L.gathered[par], 16)

                def gather_y(k, par, j):
                    s, slot = S * (2 * k + par) + j, slot_of(par, j)
                    pool.wait_ge(L.idx_staged, 2 * k + par + 1)
                    pool.wait_ge(L.rows_free, s + 1)
                    before_dma()
                    for g in range(G):
                        pool.indirect_dma_start(yrow[:, slot, g, :], None, L.table[:, :],
                                                bass.IndirectOffsetOnAxis(ap=ibuf[:, par, G * j + g:G * j + g + 1], axis=0))\
                            .then_inc(L.gathered[slot], 16)

                def scatter(k, par, j):
                    s, slot = S * (2 * k + par) + j, slot_of(par, j)
                    pool.wait_ge(L.idx2_ready, s + 1)
                    pool.wait_ge(L.sums_taken, s + 3)
                    for g in range(G):
                        if not (isinstance(s, int) and s == 0):
                            pool.wait_ge(L.scattered[g], 16 * s)
                        if g == G - 1:
                            pool.sem_inc(L.slot_done, 1)
                        before_dma()
                        v = (summed16 if L.width == D else summed)[:, slot, g, :]
                        pool.indirect_dma_start(L.acc[g][:, :], bass.IndirectOffsetOnAxis(ap=idx2[:, slot, g:g + 1], axis=0),
                                                v, None, compute_op=ALU.add).then_inc(L.scattered[g], 16)

                if L.dedupe:
                    pool.sem_inc(L.slot_done, 1)
                    pool.wait_ge(L.acc_zeroed, 16 * G)

                def body(k, par, last):
                    if L.layer == 1:
                        for j in range(S):
                            if L.gathers and not (last and j == S - 1):
                                nk, npar, nj = (k, par, j + 1) if j < S - 1 else (k + par, 1 - par, 0)
                                gather_y(nk, npar, nj)
                            scatter(k, par, j)
                        return
                    if L.window:
                        gather(k, par)
                        return
                    if not last:
                        gather(k + par, 1 - par)
                    for j in range(S):
                        scatter(k, par, j)

                if L.gathers:
                    pool.wait_ge(*{0: (t_stored[0], 16 * (NB // 2) + 16), 1: (flag_ready, 1),
                                   2: (table_stored, 32), 3: (table_stored, 48)}[L.layer])
                    if L.layer == 0:
                        pool.wait_ge(t_stored[1], 16 * (NB // 2) + 16)
                    if L.layer == 1:
                        for s in y_stored:
                            pool.wait_ge(s, 16 * (NG // 2))
                        gather_y(0, 0, 0)
                    elif L.dedupe:
                        gather(0, 0)
                run_chunks(pool, body, peel=L.dedupe)
                if L.dedupe:
                    for g in range(G):
                        pool.wait_ge(L.scattered[g], 16 * SUP)
                    pool.sem_inc(L.loop_done, 1)

            pool.wait_ge(flag_ready, 1)
            for layer in range(4):
                either(pool, layer, edges)

        @block.scalar
        def _(act):
            act.wait_ge(cleared, 1)
            small_in = lambda o, i: act.dma_start(o, i).then_inc(weights_in, 16)
            for q, name in enumerate(("L0_gnn_loop_weight", "L1_gnn_W_msg_lin", "L1_gnn_W_upd_lin", None, "L3_gnn_root")):
                w = t["L3_gnn_b2"].rearrange("(i o) -> i o", o=D) if name is None else t[name]
                for b in range(GB):
                    small_in(wbd[D * b:D * b + D, q, D * b:D * b + D], w)
            for b in range(GB):
                small_in(ybd[D * b:D * b + D, YW * b:YW * (b + 1)], t["L1_gnn_W_msg_tp"].rearrange("i j h -> i (j h)"))
                small_in(ubd[D * b:D * b + D, 256 * b:256 * (b + 1)], t["L1_gnn_W_upd_tp"].rearrange("i h k -> i (h k)"))
            for b in range(4):
                small_in(w2bd[32 * b:32 * b + 32, D * b:D * b + D], t["L2_gnn_W2"])
            with nc.allow_non_contiguous_dma(reason="768 numbers, once"):
                small_in(wgT[:, :], t["L2_gnn_W_gcn"].rearrange("i k -> k i"))
            small_in(w1g[:, :], t["L2_gnn_W1"])
            for tile, name in ((b1g, "L2_gnn_b1"), (b2g, "L2_gnn_b2"), (bias3, "L3_gnn_bias"),
                               (gamma3, "L3_gnn_gamma"), (beta3, "L3_gnn_beta")):
                small_in(tile[:, :], t[name].partition_broadcast(P))
            for g in range(G):
                small_in(w1x[D * g:D * g + D, g, :], t["L3_gnn_W1"])
                small_in(w1x[G * D:G * D + 1, g, :], t["L3_gnn_b1"].rearrange("(a n) -> a n", a=1))
            small_in(w2x[:, :, :], t["L3_gnn_W2"].rearrange("(a k) n -> k a n", a=2))
            act.wait_ge(wc_copied, 1)
            act.dma_start(wc_dram[:, :], wc[:, :]).then_inc(wc_stored, 16)
            act.wait_ge(wc_stored, 16)
            for b in range(GB):
                act.dma_start(cbd[D * b:D * b + D, 32 * b:32 * b + 32], wc_dram[:, :]).then_inc(cbd_in, 16)

            asked = [0]

            def fn(func, o, i, scale=1.0):
                asked[0] += 1
                act.wait_ge(fn_asked, asked[0])
                act.activation(o, i, func, scale=scale).then_inc(fn_done, 1)

            fn(ACT.Sqrt, nv[1][:, :], nv[0][:, :])
            act.sem_inc(t_evA, 1)
            with act.Fori(0, NB // 2) as k:
                for par in range(2):
                    b = 2 * k + par
                    act.wait_ge(t_stored[par], 16 * k + 16)
                    for i in range(0, NPIECE, 2):
                        act.wait_ge(t_prod, NPIECE * b + i + 1)
                        act.activation(tbuf[:, par, i * PIECE:(i + 1) * PIECE].rearrange("p (a n) -> p a n", a=2),
                                       table_piece(par, i), ACT.Copy).then_inc(t_evA, 1)

            def edges(L):
                if L.dedupe:
                    act.sem_inc(L.sums_taken, 2)

                def body(k, par, last):
                    c = 2 * k + par
                    if L.layer == 0:
                        act.wait_ge(L.norm_asked, c + 1)
                        act.activation(sv[1][:, :], sv[0][:, :], ACT.Sqrt)
                        act.drain()
                        act.activation(sv[2][:, :], sv[1][:, :], ACT.Tanh, scale=SQC).then_inc(L.norm_done, 1)
                    for j in range(S):
                        s, slot = S * c + j, slot_of(par, j)
                        if L.layer == 1:
                            act.wait_ge(L.m_ready, s + 1)
                            act.wait_ge(L.sums_done, s + 1)
                            act.activation(mval[:, slot, :, :], mpre[:, slot, :, :], ACT.Silu, scale=NORM_MSG)\
                               .then_inc(L.vals_ready, 1)
                        if L.layer == 3:
                            act.wait_ge(L.ea_turned, s + 1)
                            act.activation(eaT[:, slot, :], ps[0:G * D + 1, 4, 0:P], ACT.Copy)\
                               .then_inc(L.ea_copied, 1)
                            for g in range(G):
                                ts = (par + j + g) % 2
                                act.wait_ge(L.hid_done, G * s + g + 1)
                                act.activation(hid[:, ts, :], ps[:, ts, 0:256], ACT.Relu).then_inc(L.relu_done, 1)
                        if L.dedupe:
                            act.wait_ge(L.sums_done, s + 3)
                            act.wait_ge(L.slot_done, s + 1)
                            o = (summed16 if L.width == D else summed)[:, slot, :, :]
                            act.activation(o, ps[:, 6 + slot, 0:G * L.width].rearrange("p (g w) -> p g w", g=G),
                                           ACT.Copy).then_inc(L.sums_taken, 1)

                if L.dedupe or L.layer in (0, 3):
                    run_chunks(act, body)

            act.wait_ge(flag_ready, 1)
            either(act, 0, edges)
            fn(ACT.Sqrt, nv[1][:, :], nv[0][:, :])
            fn(ACT.Sqrt, nv[1][:, :], nv[0][:, :])
            fn(ACT.Sqrt, nv[1][:, :], nv[0][:, :])
            fn(ACT.Tanh, nv[2][:, :], nv[1][:, :], SQC)
            fn(ACT.Sqrt, nv[1][:, :], nv[0][:, :])
            either(act, 1, edges)
            fn(ACT.Silu, big[:, :, :], big[:, :, :], NORM_UPD)
            fn(ACT.Sqrt, nv[1][:, :], nv[0][:, :])
            fn(ACT.Sqrt, nv[1][:, :], nv[0][:, :])
            either(act, 2, edges)
            fn(ACT.Sqrt, nv[1][:, :], nv[0][:, :])
            either(act, 3, edges)
            fn(ACT.Sqrt, bn[:, 3, :], bn[:, 2, :])

        @block.tensor
        def _(pe):
            pe.wait_ge(consts, 1)
            pe.wait_ge(base_asked, 1)
            for a, n in ((0, 512), (512, SUP - 512)):
                mm = pe.matmul(ps[:, a // 512, 0:n], first_row[:, :], rel[:, a:a + n, 0], start=True, stop=True)
            mm.then_inc(base_done, 1)
            pe.wait_ge(weights_in, 16 * WEIGHT_DMAS)
            pe.matmul(ps[0:D, 2, 0:32], wgT[:, :], w1g[:, :], start=True, stop=True).then_inc(wc_done, 1)

            def turn(par, n):
                pe.wait_ge(t_staged, n)
                pe.transpose(ps[0:K_T, 6 + par, 0:P], stg[:, par, :], ident[:, :]).then_inc(t_turned, 1)

            def column(k, par, last):
                b = 2 * k + par
                if not last:
                    turn(1 - par, b + 2)
                pe.wait_ge(t_lhs, b + 1)
                free = ((t_evD, 2 * b + 1), (t_evA, 3 * b + 1), (t_evA, 3 * b + 2), (t_evD, 2 * b + 2), (t_evA, 3 * b + 3))
                for i in range(NPIECE):
                    pe.wait_ge(*free[i])
                    half = PIECE // 2 // D
                    for a in range(2):
                        r0 = (2 * i + a) * half
                        mm = pe.matmul(table_piece(par, i)[:, a, :], lt[:, par, :],
                                       wt[:, r0:r0 + half, :].rearrange("k r o -> k (r o)"), start=True, stop=True)
                    mm.then_inc(t_prod, 1)

            turn(0, 1)
            with pe.Fori(0, NB // 2 - 1) as k:
                column(k, 0, False)
                column(k, 1, False)
            column(NB // 2 - 1, 0, False)
            column(NB // 2 - 1, 1, True)

            def sequence(name, lhs, rhs):
                base, n = SEQ[name], SEQ_COLS[name]
                pe.wait_ge(seq_ready, list(SEQ).index(name) + 1)

                def turn(g):
                    a = lhs(g)
                    pe.transpose(turn_out(g, a.shape[1]), a, ident[:, :]).then_inc(turned, 1)

                turn(0)
                for g in range(SEQ_GROUPS[name]):
                    if g + 1 < SEQ_GROUPS[name]:
                        turn(g + 1)
                    pe.wait_ge(turn_copied, base + g + 1)
                    if base + g + 1 - SEQ_SLOTS[name] > 0:
                        pe.wait_ge(product_used, base + g + 1 - SEQ_SLOTS[name])
                    kk = lhs(g).shape[1]
                    o = group_out(name, g)
                    w = xt[0:kk, g % 2, :]
                    if n < 448:
                        cols = min(n, rhs.shape[1]) if name != "gcn2" else kk // 2
                        mm = pe.matmul(o[:, 0:cols], w, rhs[0:kk, 0:cols], start=True, stop=True)
                    else:
                        for a in range(n // 448):
                            mm = pe.matmul(o[:, a, :], w, rhs[0:kk, 448 * a:448 * (a + 1)], start=True, stop=True)
                    mm.then_inc(product_done, 1)

            def group_of(a):
                return lambda g: flat(a[:, GB * g:GB * g + GB, :])

            def edges(L):
                if L.window:
                    pe.sem_inc(L.sums_done, 2)
                else:
                    pe.sem_inc(L.sums_done, 2)
                if L.pick:
                    pe.sem_inc(L.picked, 2)

                def window(k, par, j):
                    s, slot = S * (2 * k + par) + j, slot_of(par, j)
                    pe.wait_ge(L.matrix_ready, s + 1)
                    pe.wait_ge(L.vals_ready, s + 1)
                    pe.wait_ge(L.sums_taken, s + 1)
                    for g in range(G):
                        mm = pe.matmul(ps[0:VW, 6 + slot, 0:WIN], vals[:, par, G * j + g, :], onehot[:, slot, g, :],
                                       start=(g == 0), stop=(g == G - 1))
                    mm.then_inc(L.sums_done, 1)

                def add_same(k, par, j):
                    s, slot = S * (2 * k + par) + j, slot_of(par, j)
                    pe.wait_ge(L.matrix_ready, s + 1)
                    pe.wait_ge(L.vals_ready, s + 1)
                    pe.wait_ge(L.sums_taken, s + 1)
                    for g in range(G):
                        v = mval[:, slot, g, :] if L.layer == 1 else vals[:, par, G * j + g, :]
                        a = g * L.width
                        mm = pe.matmul(ps[:, 6 + slot, a:a + L.width], same[:, slot, g, :], v, start=True, stop=True)
                    mm.then_inc(L.sums_done, 1)

                def pick(k, par, j):
                    s, slot = S * (2 * k + par) + j, slot_of(par, j)
                    pe.wait_ge(L.pick_ready, s + 1)
                    pe.wait_ge(L.ywin_in[slot], 16 * slot_count(k, par, j))
                    for g in range(G):
                        a = 1024 * slot + YW * g
                        mm = pe.matmul(psf[:, a:a + YW], onehot[:, slot, g, :], ywin[:, slot, :], start=True, stop=True)
                    mm.then_inc(L.picked, 1)

                def hidden(k, par, i):
                    c, j, g = 2 * k + par, i // G, i % G
                    s, slot = S * c + j, slot_of(par, j)
                    if i == 0:
                        pe.wait_ge(L.ea_in[par], 16 * (k + 1))
                    if g == 0:
                        pe.transpose(ps[0:G * D + 1, 4, 0:P], ea[:, par, j, :], ident[:, :])\
                          .then_inc(L.ea_turned, 1)
                        pe.wait_ge(L.ea_copied, s + 1)
                    ts = (par + i) % 2
                    for a in range(2):
                        mm = pe.matmul(ps[:, ts, P * a:P * a + P], w1x[:, g, P * a:P * a + P], eaT[:, slot, :],
                                       start=True, stop=True)
                    mm.then_inc(L.hid_done, 1)

                def edge_weights(k, par, i):
                    n = TC * (2 * k + par) + i
                    ts = (par + i) % 2
                    pe.wait_ge(L.relu_done, n + 1)
                    pe.wait_ge(L.w_used, n + 1)
                    for a in range(2):
                        mm = pe.matmul(ps[:, 2 + ts, 0:256], hid[:, ts, P * a:P * a + P], w2x[:, a, :],
                                       start=(a == 0), stop=(a == 1))
                    mm.then_inc(L.w_done, 1)

                reduce = window if L.window else add_same

                def body(k, par, last):
                    if L.layer == 3:
                        ahead = L.window
                        hidden(k, par, 0)
                        for i in range(TC):
                            if i + 1 < TC and (ahead or (i + 1) % G):
                                hidden(k, par, i + 1)
                            edge_weights(k, par, i)
                            if ahead and i % G == 2 and i > G:
                                reduce(k, par, i // G - 1)
                            if not ahead and i % G == G - 1:
                                reduce(k, par, i // G)
                                if i + 1 < TC:
                                    hidden(k, par, i + 1)
                        if ahead:
                            reduce(k, par, S - 1)
                    elif L.pick:
                        pick(k, par, 0)
                        for j in range(S):
                            if j + 1 < S:
                                pick(k, par, j + 1)
                            reduce(k, par, j)
                    else:
                        for j in range(S):
                            reduce(k, par, j)

                run_chunks(pe, body)
                if L.window:
                    pe.wait_ge(L.sums_taken, SUP + 2)
                    for n in range(NB):
                        q, r = n // 14, n % 14
                        if r == 0 and q >= 2:
                            pe.wait_ge(L.agg_done, q - 1)
                        mm = pe.transpose(ps[:, q % 2, VW * r:VW * r + VW], accT[0:VW, n:n + NB * (P - 1) + 1:NB],
                                          ident[0:VW, 0:VW])
                        if r == 13:
                            mm.then_inc(L.loop_done, 1)

            pe.wait_ge(flag_ready, 1)
            either(pe, 0, edges)
            sequence("loop", group_of(htan), wbd[:, 0, :])
            sequence("table1", group_of(h), ybd[:, :])
            either(pe, 1, edges)
            sequence("msg_lin", group_of(big), wbd[:, 1, :])
            sequence("update", group_of(h), ubd[:, :])
            sequence("upd_lin", group_of(big), wbd[:, 2, :])
            pe.wait_ge(cbd_in, 16 * GB)
            either(pe, 2, edges)
            sequence("gcn1", group_of(big), cbd[:, :])
            sequence("gcn2", lambda g: flat(agg[:, 4 * g:min(4 * g + 4, NB), :]), w2bd[:, :])
            either(pe, 3, edges)
            sequence("bias_w", group_of(big), wbd[:, 3, :])
            sequence("root", group_of(h), wbd[:, 4, :])
            for n in range(2):
                pe.wait_ge(bn_asked, n + 1)
                pe.matmul(ps[:, n, 0:D], ones[:, :], bn[:, 2 * n, :], start=True, stop=True).then_inc(bn_done, 1)

        @block.vector
        def _(dve):
            tt, ts_, stt = dve.tensor_tensor, dve.tensor_scalar, dve.scalar_tensor_tensor
            asked = [0]

            def ask(ins=None):
                dve.drain()
                dve.sem_inc(fn_asked, 1)
                asked[0] += 1
                dve.wait_ge(fn_done, asked[0])

            def total(o, i, op=ALU.add):
                dve.tensor_reduce(o, i, AX.X, op)

            def each(v, d=D):
                return v.unsqueeze(2).to_broadcast([P, v.shape[1], d])

            def squares(o, i):
                tt(agg[:, :, 0:D], i, i, ALU.mult)
                dve.drain()
                total(o, agg[:, :, 0:D])
                dve.drain()

            def layer_norm():
                total(nv[0][:, :], x[:, :, :])
                dve.drain()
                ts_(nv[0][:, :], nv[0][:, :], 1.0 / D, None, ALU.mult)
                dve.drain()
                tt(h[:, :, :], x[:, :, :], each(nv[0][:, :]), ALU.subtract)
                dve.drain()
                squares(nv[0][:, :], h[:, :, :])
                ts_(nv[0][:, :], nv[0][:, :], 1.0 / D, LN_EPS, ALU.mult, ALU.add)
                ask()
                dve.reciprocal(nv[2][:, :], nv[1][:, :])
                dve.drain()
                tt(h[:, :, :], h[:, :, :], each(nv[2][:, :]), ALU.mult)
                dve.drain()
                ts_(h[:, :, :], h[:, :, :], 0.0, None, ALU.max)
                dve.drain()

            def clipped(o, i):
                ts_(o, i, MIN_NORM, None, ALU.max)

            dve.memset(x[:, :, :], 0.0)
            dve.memset(wbd[:, :, :], 0.0)
            for tile in (ybd, ubd, cbd, w2bd):
                dve.memset(tile[:, :], 0.0)
            dve.memset(w1x[:, :, :], 0.0)
            dve.memset(stg[:, :, :], 1.0)
            dve.drain()
            dve.sem_inc(cleared, 1)
            dve.wait_ge(iota_done, 3)
            dve.tensor_copy(iota[:, :], iota_i[:, :])
            dve.tensor_copy(part[:, :], part_i[:, :])
            ts_(junk[:, :], part_i[:, :], float(NP), None, ALU.add)
            ts_(mask[:, :], mask_i[:, :], float(N), None, ALU.is_lt)

            dve.wait_ge(idx_in, 48)
            stt(tix[:, :, :], src[:, :, :], float(R), tix[:, :, :], ALU.mult, ALU.add)
            dve.tensor_copy(rel[:, :, :], dst[:, :, :])
            dve.drain()
            dve.sem_inc(base_asked, 1)
            dve.wait_ge(base_done, 1)
            dve.tensor_copy(base_i[:, 0:SUP], psf[:, 0:SUP])
            ts_(base_p[:, :], psf[:, 0:SUP], part[:, 0:1], None, ALU.add)
            tt(rel[:, :, :], rel[:, :, :], psf[:, 0:SUP].unsqueeze(2).to_broadcast([P, SUP, G]), ALU.subtract)
            dve.drain()
            relf = rel[:, :, :].rearrange("p s g -> p (s g)")
            dve.tensor_reduce(range_in[:, 0:1], relf, AX.X, ALU.min, negate=True)
            dve.tensor_reduce(range_in[:, 1:2], relf, AX.X, ALU.max)
            dve.drain()
            dve.sem_inc(range_ready, 1)
            dve.wait_ge(range_reduced, 1)
            ts_(fits[:, 0:1], range_all[:, 0:1], 0.5, None, ALU.is_lt)
            ts_(fits[:, 1:2], range_all[:, 1:2], WIN - 0.5, None, ALU.is_lt)
            dve.drain()
            tt(flag[:, :], fits[:, 0:1], fits[:, 1:2], ALU.mult)
            dve.drain()
            dve.sem_inc(flag_ready, 1)
            dve.wait_ge(wc_done, 1)
            dve.tensor_copy(wc[:, :], ps[0:D, 2, 0:32]).then_inc(wc_copied, 1)

            dve.wait_ge(x_in, 32)
            layer_norm()
            squares(nv[0][:, :], h[:, :, :])
            clipped(nv[0][:, :], nv[0][:, :])
            dve.drain()
            ts_(nv[0][:, :], nv[0][:, :], C, None, ALU.mult)
            dve.drain()
            ts_(nv[1][:, :], nv[0][:, :], 1.0 / (2 * ATANH_TERMS + 1), 1.0 / (2 * ATANH_TERMS - 1), ALU.mult, ALU.add)
            dve.drain()
            for n in range(ATANH_TERMS - 2, -1, -1):
                tt(nv[1][:, :], nv[1][:, :], nv[0][:, :], ALU.mult)
                dve.drain()
                ts_(nv[1][:, :], nv[1][:, :], 1.0 / (2 * n + 1), None, ALU.add)
                dve.drain()
            tt(htan[:, :, :], h[:, :, :], each(nv[1][:, :]), ALU.mult)
            dve.drain()

            def stage(par, b):
                dve.tensor_copy(stg[:, par, 0:D].unsqueeze(1), htan[:, ds(b, 1), :]).then_inc(t_staged, 1)
                dve.wait_ge(t_turned, b + 1)
                dve.tensor_copy(lt[:, par, :], ps[0:K_T, 6 + par, 0:P]).then_inc(t_lhs, 1)

            def column(k, par, last):
                b = 2 * k + par
                if not last:
                    stage(1 - par, b + 1)
                dve.wait_ge(t_stored[par], 16 * k + 16)
                for i in range(1, NPIECE, 2):
                    dve.wait_ge(t_prod, NPIECE * b + i + 1)
                    dve.tensor_copy(tbuf[:, par, i * PIECE:(i + 1) * PIECE].rearrange("p (a n) -> p a n", a=2),
                                    table_piece(par, i)).then_inc(t_evD, 1)

            dve.sem_inc(t_evD, 1)
            stage(0, 0)
            with dve.Fori(0, NB // 2 - 1) as k:
                column(k, 0, False)
                column(k, 1, False)
            column(NB // 2 - 1, 0, False)
            column(NB // 2 - 1, 1, True)
            for s in t_stored:
                dve.wait_ge(s, 16 * (NB // 2) + 16)

            def edges(L):
                if L.gathers:
                    dve.sem_inc(L.rows_free, 2)
                if L.layer == 1:
                    dve.sem_inc(L.ea_free, 2)
                if L.window:
                    dve.sem_inc(L.sums_taken, 2)
                else:
                    dve.sem_inc(L.keys_free, 2)
                if L.layer == 3:
                    dve.sem_inc(L.w_used, 2)

                def stage_idx(k, par):
                    c = 2 * k + par
                    dve.tensor_copy(ibuf[:, par, :].rearrange("p (s g) -> p s g", g=G),
                                    L.idx[:, ds(S * c, S), :]).then_inc(L.idx_staged, 1)

                def onehots(k, par, j):
                    s, slot = S * (2 * k + par) + j, slot_of(par, j)
                    dve.wait_ge(L.sums_done, s + 1)
                    tt(onehot[:, slot, :, :], iota[:, :].unsqueeze(1).to_broadcast([P, G, WIN]),
                       rel[:, ds(s, 1), :].rearrange("p a g -> p (a g)").unsqueeze(2).to_broadcast([P, G, WIN]),
                       ALU.is_equal).then_inc(L.matrix_ready, 1)

                def add_window(k, par, j, base):
                    s, slot = S * (2 * k + par) + j, slot_of(par, j)
                    dve.wait_ge(L.sums_done, s + 3)
                    o = accT[0:VW, ds(base, WIN)]
                    tt(o, o, ps[0:VW, 6 + slot, 0:WIN], ALU.add)
                    dve.drain()
                    dve.sem_inc(L.sums_taken, 1)

                def compare(k, par, j):
                    s, slot = S * (2 * k + par) + j, slot_of(par, j)
                    dve.wait_ge(L.keys_in[slot], 16 * (2 if L.pick else 1) * slot_count(k, par, j))
                    if L.pick:
                        dve.wait_ge(L.picked, s + 1)
                        ts_(onehot[:, slot, :, :], drow[:, slot, :].rearrange("p (e g) -> p g e", g=G),
                            base_p[:, ds(s, 1)], None, ALU.is_equal).then_inc(L.pick_ready, 1)
                    dve.wait_ge(L.sums_done, s + 1)
                    key = L.key[:, ds(s, 1), :].rearrange("p a g -> p (a g)")
                    tt(same[:, slot, :, :], keys[:, slot, :].rearrange("p (e g) -> p g e", g=G),
                       key.unsqueeze(2).to_broadcast([P, G, P]), ALU.is_equal)
                    ts_(keyd[:, :], key, junk[:, 0:1], None, ALU.subtract)
                    dve.drain()
                    dve.sem_inc(L.matrix_ready, 1)
                    dve.sem_inc(L.keys_free, 1)
                    before = work[:, 0:G * P].rearrange("p (g e) -> p g e", g=G)
                    tt(before, same[:, slot, :, :], lower[:, :].unsqueeze(1).to_broadcast([P, G, P]), ALU.mult)
                    dve.drain()
                    total(cnt[:, :], before)
                    dve.drain()
                    stt(keyd[:, :], cnt[:, :], 0.5, keyd[:, :], ALU.is_lt, ALU.mult)
                    dve.drain()
                    dve.wait_ge(L.slot_done, s + 1)
                    ts_(idx2[:, slot, :], keyd[:, :], junk[:, 0:1], None, ALU.add).then_inc(L.idx2_ready, 1)
                    dve.drain()

                def values0(k, par):
                    m = rows[:, par, :, :]
                    v = vals[:, par, :, :]
                    sq = work[:, 0:TC * D].rearrange("p (t d) -> p t d", d=D)
                    n2, n, th, rn, f, q = (sv[i][:, :] for i in (3, 1, 2, 4, 5, 6))
                    tt(sq, m, m, ALU.mult)
                    dve.drain()
                    total(n2, sq)
                    dve.drain()
                    clipped(sv[0][:, :], n2)
                    dve.drain()
                    dve.sem_inc(L.norm_asked, 1)
                    dve.wait_ge(L.norm_done, 2 * k + par + 1)
                    dve.reciprocal(rn, n)
                    dve.drain()
                    stt(f, th, 1.0 / SQC, rn, ALU.mult, ALU.mult)
                    dve.drain()
                    tt(q, f, f, ALU.mult)
                    dve.drain()
                    tt(q, q, n2, ALU.mult)
                    dve.drain()
                    ts_(q, q, -C, 1.0, ALU.mult, ALU.add)
                    dve.drain()
                    ts_(q, q, EPS, None, ALU.add)
                    dve.drain()
                    dve.reciprocal(rn, q)
                    dve.drain()
                    ts_(v[:, :, D:D + 1].rearrange("p t a -> p (t a)"), rn, 2.0, None, ALU.mult)
                    stt(f, rn, 2.0, f, ALU.mult, ALU.mult)
                    dve.drain()
                    tt(v[:, :, 0:D], m, f.unsqueeze(2).to_broadcast([P, TC, D]), ALU.mult)
                    dve.drain()
                    dve.sem_inc(L.vals_ready, S)
                    dve.sem_inc(L.rows_free, 1)

                def values1(k, par, j):
                    s, slot = S * (2 * k + par) + j, slot_of(par, j)
                    if L.pick:
                        dve.wait_ge(L.picked, s + 3)
                        y = psf[:, 1024 * slot:1024 * slot + G * YW]
                    else:
                        dve.wait_ge(L.gathered[slot], 16 * G * slot_count(k, par, j))
                        y = yrow[:, slot, :, :].rearrange("p g w -> p (g w)")
                    w = work[:, 0:G * YW]
                    tt(w.rearrange("p (a h) -> p a h", h=D), y.rearrange("p (a h) -> p a h", h=D),
                       ea8[:, par, G * j:G * j + G, :].rearrange("p g j -> p (g j)").unsqueeze(2).to_broadcast([P, G * DE, D]),
                       ALU.mult)
                    dve.drain()
                    if L.gathers:
                        dve.sem_inc(L.rows_free, 1)
                    total(mpre[:, slot, :, :], w.rearrange("p (g j h) -> p g h j", j=DE, h=D))
                    dve.drain()
                    dve.sem_inc(L.m_ready, 1)
                    if j == S - 1:
                        dve.sem_inc(L.ea_free, 1)

                def values3(k, par, j):
                    n = TC * (2 * k + par) + G * j
                    for g in range(G):
                        dve.wait_ge(L.w_done, n + g + 1)
                        tt(work[:, 256 * g:256 * g + 256].rearrange("p (i o) -> p i o", o=D),
                           ps[:, 2 + (par + j + g) % 2, 0:256].rearrange("p (i o) -> p i o", o=D),
                           rows[:, par, G * j + g, :].unsqueeze(2).to_broadcast([P, D, D]), ALU.mult).then_inc(L.w_used, 1)
                    dve.drain()
                    total(vals[:, par, G * j:G * j + G, 0:D],
                          work[:, :].rearrange("p (g i o) -> p g o i", i=D, o=D))
                    dve.tensor_copy(vals[:, par, G * j:G * j + G, D:2 * D], rows[:, par, G * j:G * j + G, :])
                    dve.drain()
                    dve.sem_inc(L.vals_ready, 1)
                    if j == S - 1:
                        dve.sem_inc(L.rows_free, 1)

                def body(k, par, last):
                    c = 2 * k + par
                    if L.gathers and not last:
                        stage_idx(k + par, 1 - par)
                    if L.window:
                        _, bases = nc.values_load_multi_w_load_instructions(
                            base_i[0:1, ds(S * c, S)], engines=[dve.engine], min_val=0, max_val=NP)
                    if L.layer == 1:
                        dve.wait_ge(L.ea_in[par], 16 * (k + 1))
                    else:
                        dve.wait_ge(L.gathered[par], 16 * TC * (k + 1))
                    if L.layer == 0:
                        values0(k, par)
                    if L.layer == 2:
                        dve.tensor_copy(vals[:, par, :, 0:D], rows[:, par, :, :])
                        dve.drain()
                        dve.sem_inc(L.vals_ready, S)
                        dve.sem_inc(L.rows_free, 1)
                    for j in range(S):
                        if L.window:
                            onehots(k, par, j)
                        else:
                            compare(k, par, j)
                        if L.layer == 1:
                            values1(k, par, j)
                        if L.layer == 3:
                            values3(k, par, j)
                        if L.window and j:
                            add_window(k, par, j - 1, bases[j - 1])
                    if L.window:
                        add_window(k, par, S - 1, bases[S - 1])

                if L.gathers:
                    stage_idx(0, 0)
                run_chunks(dve, body)

                if L.window:
                    for q in range(NB // 14):
                        dve.wait_ge(L.loop_done, q + 1)
                        dve.tensor_copy(flat(agg[:, 14 * q:14 * q + 14, :]), ps[:, q % 2, 0:14 * VW]).then_inc(L.agg_done, 1)
                    dve.drain()
                else:
                    w = L.width * NB
                    o = agg[:, :, 0:L.width]
                    parts = [accT[:, i * w:(i + 1) * w].rearrange("p (b w) -> p b w", b=NB) for i in range(4)]
                    dve.wait_ge(L.acc_loaded, 64)
                    tt(o, parts[0], parts[1], ALU.add)
                    dve.drain()
                    tt(o, o, parts[2], ALU.add)
                    dve.drain()
                    tt(o, o, parts[3], ALU.add)
                    dve.drain()
                    dve.sem_inc(L.agg_done, 1)
                    dve.wait_ge(L.acc_loaded, 80)
                    tt(o, o, parts[0], ALU.add)
                    dve.drain()

            def begin_edges():
                dve.memset(accT[:, :], 0.0)
                dve.drain()
                dve.sem_inc(acc_cleared, 1)

            def sequence(name, lhs_cols, use):
                base = SEQ[name]
                dve.drain()
                dve.sem_inc(seq_ready, 1)

                def copy(g):
                    dve.wait_ge(turned, base + g + 1)
                    dve.tensor_copy(xt[0:lhs_cols(g), g % 2, :], turn_out(g, lhs_cols(g))).then_inc(turn_copied, 1)

                copy(0)
                for g in range(SEQ_GROUPS[name]):
                    if g + 1 < SEQ_GROUPS[name]:
                        copy(g + 1)
                    dve.wait_ge(product_done, base + g + 1)
                    use(g, group_out(name, g))
                    dve.drain()
                    dve.sem_inc(product_used, 1)
                dve.drain()

            cols7 = lambda g: GB * D

            def into(tile, scale=1.0, add=None):
                def use(g, o):
                    dest = flat(tile[:, GB * g:GB * g + GB, :])
                    if add is None:
                        ts_(dest, o, scale, None, ALU.mult)
                    else:
                        stt(dest, o, scale, flat(add[:, GB * g:GB * g + GB, :]), ALU.mult, ALU.add)
                return use

            begin_edges()
            dve.memset(vals[:, :, :, :], 0.0)
            dve.drain()
            for par in range(2):
                dve.memset(vals[:, par, :, D + 1:D + 2], 1.0)
            dve.drain()
            either(dve, 0, edges)

            one_over = dve.reciprocal
            dve.tensor_copy(deg[:, :], agg[:, :, D + 1:D + 2].rearrange("p b a -> p (b a)"))
            dve.drain()
            ts_(nv[0][:, :], deg[:, :], 1.0, None, ALU.max)
            ask()
            one_over(nv[2][:, :], nv[1][:, :])
            dve.drain()
            tt(nv[3][:, :], deg[:, :], nv[2][:, :], ALU.mult)
            dve.drain()
            ts_(nv[3][:, :], nv[3][:, :], EPS, None, ALU.add)
            dve.drain()
            one_over(nv[4][:, :], nv[3][:, :])
            dve.drain()
            tt(nv[2][:, :], nv[2][:, :], nv[4][:, :], ALU.mult)
            dve.drain()
            tt(nv[3][:, :], nv[2][:, :], agg[:, :, D:D + 1].rearrange("p b a -> p (b a)"), ALU.mult)
            dve.drain()
            ts_(nv[3][:, :], nv[3][:, :], EPS, None, ALU.add)
            dve.drain()
            one_over(nv[4][:, :], nv[3][:, :])
            dve.drain()
            tt(nv[2][:, :], nv[2][:, :], nv[4][:, :], ALU.mult)
            dve.drain()
            tt(big[:, :, :], agg[:, :, 0:D], each(nv[2][:, :]), ALU.mult)
            dve.drain()
            squares(nv[0][:, :], big[:, :, :])
            clipped(nv[0][:, :], nv[0][:, :])
            ask()
            one_over(nv[2][:, :], nv[1][:, :])
            dve.drain()
            ts_(nv[2][:, :], nv[2][:, :], (1.0 - BALL_EPS) / SQC, 1.0, ALU.mult, ALU.min)
            dve.drain()
            tt(big[:, :, :], big[:, :, :], each(nv[2][:, :]), ALU.mult)
            sequence("loop", cols7, into(htan))
            squares(nv[0][:, :], htan[:, :, :])
            clipped(nv[0][:, :], nv[0][:, :])
            ask()
            ask()
            one_over(nv[3][:, :], nv[1][:, :])
            dve.drain()
            stt(nv[3][:, :], nv[2][:, :], 1.0 / SQC, nv[3][:, :], ALU.mult, ALU.mult)
            dve.drain()
            tt(htan[:, :, :], htan[:, :, :], each(nv[3][:, :]), ALU.mult)
            dve.drain()
            x2, y2, xy, a, b, den = (v[:, :] for v in nv)
            squares(x2, big[:, :, :])
            squares(y2, htan[:, :, :])
            tt(agg[:, :, 0:D], big[:, :, :], htan[:, :, :], ALU.mult)
            dve.drain()
            total(xy, agg[:, :, 0:D])
            dve.drain()
            ts_(xy, xy, 2 * C, 1.0, ALU.mult, ALU.add)
            ts_(b, x2, -C, 1.0, ALU.mult, ALU.add)
            tt(den, x2, y2, ALU.mult)
            dve.drain()
            stt(a, y2, C, xy, ALU.mult, ALU.add)
            stt(den, den, C * C, xy, ALU.mult, ALU.add)
            dve.drain()
            ts_(den, den, MIN_NORM, None, ALU.max)
            tt(big[:, :, :], big[:, :, :], each(a), ALU.mult)
            tt(htan[:, :, :], htan[:, :, :], each(b), ALU.mult)
            dve.drain()
            one_over(x2, den)
            tt(big[:, :, :], big[:, :, :], htan[:, :, :], ALU.add)
            dve.drain()
            tt(big[:, :, :], big[:, :, :], each(x2), ALU.mult)
            dve.drain()
            tt(x[:, :, :], x[:, :, :], big[:, :, :], ALU.add)
            dve.drain()

            layer_norm()

            def to_table(g, o):
                if g >= 2:
                    dve.wait_ge(y_stored[g % 2], 16 * (g // 2))
                dve.tensor_copy(gout[:, (g % 2) * 896:(g % 2 + 1) * 896].rearrange("p (a n) -> p a n", a=2), o)

            sequence("table1", cols7, to_table)
            for s in y_stored:
                dve.wait_ge(s, 16 * (NG // 2))
            begin_edges()
            either(dve, 1, edges)
            dve.tensor_copy(big[:, :, :], agg[:, :, 0:D])
            sequence("msg_lin", cols7, into(htan, NORM_LIN))

            def update(g, o):
                s = htan[:, GB * g:GB * g + GB, :].rearrange("p b h -> p (b h)")
                w = gout[:, :]
                for q in range(4):
                    tt(w[:, 448 * q:448 * (q + 1)].rearrange("p (a k) -> p a k", k=D),
                       o[:, q, :].rearrange("p (a k) -> p a k", k=D),
                       s[:, 28 * q:28 * (q + 1)].unsqueeze(2).to_broadcast([P, 28, D]), ALU.mult)
                dve.drain()
                total(big[:, GB * g:GB * g + GB, :], w.rearrange("p (b h k) -> p b k h", h=D, k=D))

            sequence("update", cols7, update)
            ask()
            sequence("upd_lin", cols7, into(htan, NORM_LIN, h))
            tt(x[:, :, :], x[:, :, :], htan[:, :, :], ALU.add)
            dve.drain()

            layer_norm()
            ts_(nv[0][:, :], deg[:, :], 1.0, None, ALU.add)
            ask()
            one_over(deg[:, :], nv[1][:, :])
            dve.drain()
            tt(big[:, :, :], h[:, :, :], each(deg[:, :]), ALU.mult)
            dve.drain()
            dve.sem_inc(table_ready, 1)
            begin_edges()
            dve.memset(vals[:, :, :, :], 0.0)
            dve.drain()
            either(dve, 2, edges)
            tt(big[:, :, :], big[:, :, :], agg[:, :, 0:D], ALU.add)
            dve.drain()
            tt(big[:, :, :], big[:, :, :], each(deg[:, :]), ALU.mult)

            def relu_bias(g, o):
                hidden = agg[:, GB * g:GB * g + GB, :]
                tt(hidden, o.rearrange("p (b k) -> p b k", b=GB), b1g[:, :].unsqueeze(1).to_broadcast([P, GB, 32]), ALU.add)
                dve.drain()
                ts_(hidden, hidden, 0.0, None, ALU.max)

            sequence("gcn1", cols7, relu_bias)

            def residual(g, o):
                n = min(4, NB - 4 * g)
                tt(htan[:, 4 * g:4 * g + n, :], o[:, 0:n * D].rearrange("p (b k) -> p b k", k=D),
                   b2g[:, :].unsqueeze(1).to_broadcast([P, n, D]), ALU.add)

            sequence("gcn2", lambda g: 32 * min(4, NB - 4 * g), residual)
            tt(htan[:, :, :], htan[:, :, :], h[:, :, :], ALU.add)
            dve.drain()
            tt(x[:, :, :], x[:, :, :], htan[:, :, :], ALU.add)
            dve.drain()

            layer_norm()
            dve.sem_inc(table_ready, 1)
            begin_edges()
            dve.memset(ea[:, :, :, :], 1.0)
            dve.drain()
            either(dve, 3, edges)
            dve.tensor_copy(htan[:, :, :], agg[:, :, 0:D])
            dve.tensor_copy(big[:, :, :], agg[:, :, D:2 * D])
            sequence("bias_w", cols7, into(htan, 1.0, htan))
            sequence("root", cols7, into(big, 1.0, htan))
            tt(big[:, :, :], big[:, :, :], bias3[:, :].unsqueeze(1).to_broadcast([P, NB, D]), ALU.add)
            dve.drain()

            def batch_sum(n, i):
                tt(htan[:, :, :], i, each(mask[:, :]), ALU.mult)
                dve.drain()
                total(bn[:, 2 * n, :], htan[:, :, :].rearrange("p b d -> p d b"))
                dve.drain()
                dve.sem_inc(bn_asked, 1)
                dve.wait_ge(bn_done, n + 1)
                ts_(bn[:, 1, :], ps[:, n, 0:D], 1.0 / N, None, ALU.mult)
                dve.drain()

            def every(v):
                return v.unsqueeze(1).to_broadcast([P, NB, D])

            batch_sum(0, big[:, :, :])
            tt(big[:, :, :], big[:, :, :], every(bn[:, 1, :]), ALU.subtract)
            dve.drain()
            tt(h[:, :, :], big[:, :, :], big[:, :, :], ALU.mult)
            dve.drain()
            batch_sum(1, h[:, :, :])
            ts_(bn[:, 2, :], bn[:, 1, :], LN_EPS, None, ALU.add)
            ask()
            dve.reciprocal(bn[:, 4, :], bn[:, 3, :])
            dve.drain()
            tt(bn[:, 4, :], bn[:, 4, :], gamma3[:, :], ALU.mult)
            dve.drain()
            tt(big[:, :, :], big[:, :, :], every(bn[:, 4, :]), ALU.mult)
            dve.drain()
            tt(big[:, :, :], big[:, :, :], every(beta3[:, :]), ALU.add)
            dve.drain()
            stt(x[:, :, :], big[:, :, :], 0.0, x[:, :, :], ALU.max, ALU.add)
            dve.drain()
            dve.sem_inc(out_ready, 1)


_INS = ["x", "src", "dst", "edge_attr_16", "edge_attr_8", "edge_type_230", "node_vec1",
        "L0_gnn_rel_weight", "L0_gnn_loop_weight", "L0_gnn_rel_emb",
        "L1_gnn_W_msg_tp", "L1_gnn_W_msg_lin", "L1_gnn_W_upd_tp", "L1_gnn_W_upd_lin",
        "L2_gnn_W_gcn", "L2_gnn_W1", "L2_gnn_b1", "L2_gnn_W2", "L2_gnn_b2",
        "L3_gnn_W1", "L3_gnn_b1", "L3_gnn_W2", "L3_gnn_b2", "L3_gnn_root", "L3_gnn_bias",
        "L3_gnn_gamma", "L3_gnn_beta"]


def kernel(**inputs):
    import numpy as _np
    import concourse.bacc as _bacc
    from concourse import mybir as _mybir
    from concourse.bass_utils import run_bass_kernel_spmd as _run

    nc = _bacc.Bacc("TRN2", target_bir_lowering=False, num_devices=1)
    arrays, args = {}, {}
    for name in _INS:
        a = _np.ascontiguousarray(inputs[name])
        arrays[f"in_{name}"] = a
        args[name] = nc.dram_tensor(f"in_{name}", a.shape, _mybir.dt.from_np(a.dtype), kind="ExternalInput").ap()
    out = nc.dram_tensor("out_x", (N, D), F32, kind="ExternalOutput").ap()
    gnn_kernel(nc, args, out)
    r = _run(nc, [arrays], core_ids=[0])
    return r.results[0]["out_x"]
```

```python
from contextlib import ExitStack

import concourse.bass as bass
from concourse import mybir

ALU = mybir.AluOpType
ACT = mybir.ActivationFunctionType
AX = mybir.AxisListType
F32 = mybir.dt.float32
I32 = mybir.dt.int32
BF16 = mybir.dt.bfloat16
MAX = bass.bass_isa.ReduceOp.max
ds = bass.ds

P = 128
N = 12500
E = 400000
D = 16
R = 230
DE = 8
NB = -(-N // P)
NP = NB * P
GB = 7
NG = NB // GB
G = 5
SUP = E // (P * G)
S = 5
TC = S * G
CH = SUP // S
PAIRS = CH // 2
WIN = 128
ACCN = NP + P
VW = 32
RIGHT = "hhmmhl"
K6 = 6 * D + 3
HROW = D + 3 * D // 2
TROW = R * D
PIECE = 2 * 368
NPIECE = TROW // PIECE
C = 0.01
SQC = 0.1
EPS = 1e-6
MIN_NORM = 1e-10
BALL_EPS = 1e-5
LN_EPS = 1e-5
NORM_MSG = 1.0 / float((D * DE) ** 0.5)
NORM_UPD = 1.0 / D
NORM_LIN = 0.25
FAST, GENERAL = "sorted", "general"
W_BANK = (2, 3, 5, 2, 3)
W_AGO = (2, 2, 5, 3, 3)
YW = D * DE
ATANH_TERMS = 10
WEIGHT_DMAS = 5 * GB + 2 * GB + 4 + 2 + 5 + 6 + 3 + 1
SEQS = [("loop", NG, GB * D, 2), ("table1", NG, GB * YW, 2), ("msg_lin", NG, GB * D, 2), ("update", NG, GB * 256, 1),
        ("upd_lin", NG, GB * D, 2), ("gcn1", NG, GB * 32, 2), ("gcn2", -(-NB // 4), 4 * D, 2),
        ("bias_w", NG, GB * D, 2), ("root", NG, GB * D, 2)]
SEQ_GROUPS = {n: g for n, g, _, _ in SEQS}
SEQ_COLS = {n: c for n, _, c, _ in SEQS}
SEQ_SLOTS = {n: s for n, _, _, s in SEQS}
SEQ = {n: sum(g for _, g, _, _ in SEQS[:i]) for i, (n, _, _, _) in enumerate(SEQS)}


def gnn_kernel(nc, t, out):
    ctx = ExitStack()
    with ctx:
        def sb(name, shape, dt=F32):
            return ctx.enter_context(nc.sbuf_tensor(name, shape, dt))

        def sem(name):
            return ctx.enter_context(nc.semaphore(name))

        def flat(a):
            return a.rearrange("p b w -> p (b w)")

        msg_tab = nc.dram_tensor("message_table", [NP * R, D], F32)
        y_tab = nc.dram_tensor("layer1_table", [NP + WIN, YW], F32)
        z_tab = nc.dram_tensor("layer2_table", [NP, D], F32)
        h_tab = nc.dram_tensor("layer3_table", [NP, HROW], F32)
        wc_dram = nc.dram_tensor("layer2_weight", [D, 32], F32)
        acc16 = [nc.dram_tensor(f"acc16_{g}", [ACCN, D], F32) for g in range(G)]
        acc32 = [nc.dram_tensor(f"acc32_{g}", [ACCN, VW], F32) for g in range(G)]

        x = sb("x", [P, NB, D])
        h = sb("h", [P, NB, D])
        src = sb("src", [P, SUP, G], I32)
        dst = sb("dst", [P, SUP, G], I32)
        tix = sb("tix", [P, SUP, G], I32)
        rel = sb("rel", [P, SUP, G])
        base_i = sb("base_i", [P, SUP + 3], I32)
        base_p = sb("base_p", [P, SUP])
        accT = sb("accT", [P, ACCN])
        agg = sb("agg", [P, NB, VW])
        htan = sb("htan", [P, NB, D])
        ident = sb("ident", [P, P])
        first_row = sb("first_row", [P, P])
        ones = sb("ones", [P, P])
        iota = sb("iota", [P, WIN])
        part_i = sb("part_i", [P, 1], I32)
        part = sb("part", [P, 1])
        junk = sb("junk", [P, 1])
        mask = sb("mask", [P, NB])
        range_in = sb("range_in", [P, 2])
        range_all = sb("range_all", [P, 2])
        fits = sb("fits", [P, 2])
        flag = sb("flag", [P, 1], I32)
        deg = sb("deg", [P, NB])
        wt_space = sb("wt_space", [P, TROW])
        ident_b = sb("ident_b", [P, P], BF16)
        fold = sb("fold", [3 * VW, VW])
        in_h, in_m, in_l = sb("in_h", [P, 1]), sb("in_m", [P, 1]), sb("in_l", [P, 1])
        band = [sb(f"band{i}", [P, 6]) for i in range(2)]
        pow_i = sb("pow_i", [P, 2], I32)
        wbd = sb("wbd", [P, 5, GB * D])
        ybd = sb("ybd", [P, GB * YW])
        ubd = sb("ubd", [P, GB * 256])
        cbd = sb("cbd", [P, GB * 32])
        w2bd = sb("w2bd", [P, 4 * D])
        wgT = sb("wgT", [48, D])
        w1g = sb("w1g", [48, 32])
        wc = sb("wc", [D, 32])
        b1g = sb("b1g", [P, 32])
        b2g = sb("b2g", [P, D])
        bias3 = sb("bias3", [P, D])
        gamma3 = sb("gamma3", [P, D])
        beta3 = sb("beta3", [P, D])
        w1 = sb("w1", [K6, 256], BF16)
        w2x = sb("w2x", [P, 2, 256])
        nv = [sb(f"nv{i}", [P, NB]) for i in range(6)]
        big = sb("big", [P, NB, D])
        xt = sb("xt", [P, 2, P])
        gout = sb("gout", [P, GB * 256])
        bn = sb("bn", [P, 8, D])
        ibuf = sb("ibuf", [P, 2, TC], I32)
        row_space = sb("row_space", [P, 2 * TC * HROW])
        rows = row_space[:, 0:2 * TC * D].rearrange("p (a t w) -> p a t w", a=2, t=TC)
        rows3 = row_space[:, :].rearrange("p (a t w) -> p a t w", a=2, t=TC)
        parts3 = row_space[:, :].bitcast(BF16).rearrange("p (a t w) -> p a t w", a=2, t=TC)
        w1raw = row_space[0:K6, 0:256]
        iota_i = row_space[:, 256:256 + WIN].bitcast(I32)
        mask_i = row_space[:, 384:384 + NB].bitcast(I32)
        cnt = sb("cnt", [P, G])
        keyd = sb("keyd", [P, G])
        idx2 = sb("idx2", [P, 2, G], I32)
        summed = sb("summed", [P, 2, G * VW + G])
        ea6 = sb("ea6", [P, 2, TC, K6], BF16)
        sv = [sb(f"sv{i}", [P, TC]) for i in range(8)]
        mpre = sb("mpre", [P, 2, G, D])
        mval = sb("mval", [P, 2, G, D + 1])
        agg_space = flat(agg[:, :, :])
        work = agg_space[:, 0:G * 256]
        vals = agg_space[:, G * 256:G * 256 + 2 * TC * VW].rearrange("p (a t w) -> p a t w", a=2, t=TC)
        onehot = gout[:, 0:2 * G * WIN].rearrange("p (a g n) -> p a g n", a=2, g=G)
        picks = gout[:, 0:2 * G * P].rearrange("p (a n) -> p a n", a=2)
        big_space = flat(big[:, :, :])
        hid = big_space[:, 0:512].rearrange("p (a n) -> p a n", a=2)
        vparts = big_space[:, 512:992].bitcast(BF16).rearrange("p (a g q w) -> p a g q w", a=2, g=G, q=3)
        msg = big_space[:, 992:992 + G * D].rearrange("p (g w) -> p g w", g=G)
        same = wt_space[:, 0:2 * G * P].rearrange("p (a g n) -> p a g n", a=2, g=G)
        keys = wt_space[:, 2 * G * P:4 * G * P].bitcast(I32).rearrange("p (a n) -> p a n", a=2)
        o0 = 4 * G * P
        eaT = wt_space[0:K6, o0:o0 + G * P].bitcast(BF16).rearrange("p (a n) -> p a n", a=2)
        rest = wt_space[:, o0 + G * P:o0 + G * P + TC * D].rearrange("p (t w) -> p t w", t=TC)
        tix_space = flat(tix[:, :, :])
        tix_f = tix_space.bitcast(F32)
        drow = tix_space[:, 0:2 * G * P].rearrange("p (a n) -> p a n", a=2)
        o1 = 2 * G * P
        ea8 = tix_f[:, o1:o1 + 2 * TC * DE].rearrange("p (a t w) -> p a t w", a=2, t=TC)
        o2 = o1 + 2 * TC * DE
        ywin = tix_f[:, o2:o2 + 2 * YW].rearrange("p (a n) -> p a n", a=2)
        o3 = o2 + 2 * YW
        ea = tix_f[:, o3:o3 + 2 * TC * D].rearrange("p (a t w) -> p a t w", a=2, t=TC)
        onehot_b = gout[:, 0:G * WIN].bitcast(BF16).rearrange("p (a g n) -> p a g n", a=2, g=G)
        lt = xt[0:K6, 0, :].bitcast(BF16).rearrange("p (a n) -> p a n", a=2)
        stg = xt[:, 1, 0:K6].bitcast(BF16).rearrange("p (a n) -> p a n", a=2)
        htan6 = accT[:, 2 * TROW:ACCN].bitcast(BF16)[:, 0:NB * K6].rearrange("p (b k) -> p b k", b=NB)
        wt = wt_space[0:K6, :]
        wt6 = agg_space[0:K6, 0:TROW // 2].bitcast(BF16)
        h_rows = accT[:, 0:NB * HROW].rearrange("p (b w) -> p b w", b=NB)
        h_parts = accT[:, 0:NB * HROW].bitcast(BF16).rearrange("p (b w) -> p b w", b=NB)
        tbuf = accT[:, 0:2 * TROW].rearrange("p (a n) -> p a n", a=2)
        yrow = accT[:, 0:2 * G * YW].rearrange("p (a g w) -> p a g w", a=2, g=G)

        ps = ctx.enter_context(nc.psum_tensor("ps", [P, 8, 512], F32))
        psf = ps[:, :, :].rearrange("p b n -> p (b n)")

        cleared, consts, x_in, weights_in, idx_in, iota_done = (
            sem("cleared"), sem("consts"), sem("x_in"), sem("weights_in"), sem("idx_in"), sem("iota_done"))
        rel_in = sem("rel_in")
        base_asked, base_done = sem("base_asked"), sem("base_done")
        range_ready, range_reduced, flag_ready = sem("range_ready"), sem("range_reduced"), sem("flag_ready")
        fn_asked, fn_done = sem("fn_asked"), sem("fn_done")
        seq_ready, turned, turn_copied, product_done, product_used = (
            sem("seq_ready"), sem("turned"), sem("turn_copied"), sem("product_done"), sem("product_used"))
        t_staged, t_turned, t_lhs, t_prod, t_evA, t_evD = (
            sem("t_staged"), sem("t_turned"), sem("t_lhs"), sem("t_prod"), sem("t_evA"), sem("t_evD"))
        t_stored = [sem("t_stored0"), sem("t_stored1")]
        acc_cleared = sem("acc_cleared")
        table_ready, table_stored = sem("table_ready"), sem("table_stored")
        y_stored = [sem("y_stored0"), sem("y_stored1")]
        wc_done, wc_copied, wc_stored, cbd_in = sem("wc_done"), sem("wc_copied"), sem("wc_stored"), sem("cbd_in")
        bn_asked, bn_done = sem("bn_asked"), sem("bn_done")
        out_ready, out_stored = sem("out_ready"), sem("out_stored")
        pool_turn = sem("pool_turn")

        loop_sems = {}

        class Loop:

            def __init__(self, layer, mode):
                self.layer, self.mode = layer, mode
                self.window = layer != 1 and mode == FAST
                self.in_parts = layer == 3 and mode == FAST
                self.dedupe = not self.window
                self.pick = layer == 1 and mode == FAST
                self.gathers = not self.pick
                self.width = D if layer == 1 else VW
                self.step = D + 1 if layer == 1 else VW
                self.acc = acc16 if layer == 1 else acc32
                self.key = src if layer == 1 else dst
                self.key_dram = t["src"] if layer == 1 else t["dst"]
                self.idx = {0: tix, 1: dst, 2: src, 3: src}[layer]
                self.table = {0: msg_tab, 1: y_tab, 2: z_tab, 3: h_tab}[layer]

                def s(name):
                    name = f"L{layer}_{name}"
                    if name not in loop_sems:
                        loop_sems[name] = sem(name)
                    return loop_sems[name]

                if self.gathers:
                    self.idx_staged = s("idx_staged")
                    self.gathered = [s("gathered0"), s("gathered1")]
                    self.rows_free = s("rows_free")
                self.vals_ready = s("vals_ready")
                if self.window:
                    self.matrix_ready, self.sums_done, self.sums_taken = (
                        s("matrix_ready"), s("sums_done"), s("sums_taken"))
                    self.loop_done, self.agg_done = s("loop_done"), s("agg_done")
                else:
                    self.keys_in = [s("keys_in0"), s("keys_in1")]
                    self.keys_free, self.matrix_ready, self.sums_done, self.sums_taken = (
                        s("keys_free"), s("matrix_ready"), s("sums_done"), s("sums_taken"))
                    self.idx2_ready, self.slot_done = s("idx2_ready"), s("slot_done")
                    self.scattered = [s(f"scattered{g}") for g in range(G)]
                    self.acc_zeroed, self.loop_done, self.acc_loaded, self.agg_done = (
                        s("acc_zeroed"), s("loop_done"), s("acc_loaded"), s("agg_done"))
                if layer == 0:
                    self.norm_asked, self.norm_done = s("norm_asked"), s("norm_done")
                if layer in (1, 3):
                    self.ea_in = [s("ea_in0"), s("ea_in1")]
                if layer == 1:
                    self.ea_free, self.m_ready = s("ea_free"), s("m_ready")
                if self.pick:
                    self.pick_ready, self.picked = s("pick_ready"), s("picked")
                    self.ywin_in = [s("ywin_in0"), s("ywin_in1")]
                if layer == 3:
                    self.ea_h, self.ea_rest, self.ea_ready, self.x_ready = s("ea_h"), s("ea_rest"), s("ea_ready"), s("x_ready")
                    self.ea_turned, self.ea_copied, self.hid_done, self.relu_done, self.w_done, self.w_used = (
                        s("ea_turned"), s("ea_copied"), s("hid_done"), s("relu_done"), s("w_done"), s("w_used"))

        loops = {(l, m): Loop(l, m) for l in range(4) for m in (FAST, GENERAL)}

        def by_tile(a):
            return a.rearrange("(s p g) -> p s g", p=P, g=G)

        def by_tile_rows(a):
            return a.rearrange("(s p g) w -> p s (g w)", p=P, g=G)

        def node_rows(a):
            return a[0:NP, :].rearrange("(p b) w -> p (b w)", p=P)

        def run_chunks(eng, body, peel=False):
            if peel:
                body(0, 0, False)
                body(0, 1, False)
            with eng.Fori(int(peel), PAIRS) as k:
                body(k, 0, False)
                body(k, 1, False)
            body(PAIRS, 0, True)

        def either(eng, layer, fn):
            fit = eng.value_load(flag[0:1, 0:1], min_val=0, max_val=1)
            with eng.If(fit > 0):
                fn(loops[layer, FAST])
            with eng.Else():
                fn(loops[layer, GENERAL])

        def slot_of(par, j):
            return (S * par + j) % 2

        def slot_count(k, par, j):
            return S * k + (S * par + j) // 2 + 1

        def table_piece(par, i):
            q = 2 * ((NPIECE * par + i) % 2)
            return ps[:, q:q + 2, 0:PIECE // 2]

        def ea_blocks(par, first):
            return ea6[:, par, :, 0:4 * D].rearrange("p t (a w) -> p t a w", a=2)[:, :, :, first * D:first * D + D]

        def group_out(name, g):
            n, slots = SEQ_COLS[name], SEQ_SLOTS[name]
            first = 2 * (g % slots)
            banks = max(1, n // 448)
            if banks == 1:
                return ps[:, first, 0:n]
            return ps[:, first:first + banks, 0:448]

        def turn_out(g, cols):
            return ps[0:cols, 6 + g % 2, 0:P]

        block = ctx.enter_context(nc.Block())

        @block.sync
        def _(sp):
            full = (N // NB) * NB
            last = N // NB
            flat_x = t["x"].rearrange("n d -> (n d)")
            sp.wait_ge(cleared, 1)
            sp.dma_start(flat(x[0:last, :, :]), t["x"][0:full, :].rearrange("(p b) d -> p (b d)", b=NB)).then_inc(x_in, 16)
            sp.dma_start(flat(x[last:last + 1, 0:N - full, :]),
                         flat_x[full * D:N * D].rearrange("(a n) -> a n", a=1)).then_inc(x_in, 16)
            sp.dma_start(wt[0:D, :].rearrange("k (r o) -> k r o", o=D),
                         t["L0_gnn_rel_weight"].rearrange("r i o -> i r o")).then_inc(rel_in, 16)
            for q in range(3):
                sp.dma_start(wt[6 * D + q:6 * D + q + 1, :], t["L0_gnn_rel_emb"].rearrange("(a r) o -> a (r o)", a=1)).then_inc(rel_in, 16)
            sp.wait_ge(rel_in, 64)
            for q in range(1, 6):
                sp.dma_start(wt[D * q:D * q + D, :], wt[0:D, :]).then_inc(rel_in, 16)
            for tile, name in ((dst, "dst"), (src, "src"), (tix, "edge_type_230")):
                sp.dma_start(tile[:, :, :], by_tile(t[name])).then_inc(idx_in, 16)

            for s in t_stored:
                sp.sem_inc(s, 16)
            tdram = msg_tab[:, :].rearrange("(p b r) w -> p b (r w)", p=P, b=NB)
            with sp.Fori(0, NB // 2) as k:
                for par in range(2):
                    b = 2 * k + par
                    sp.wait_ge(t_evA, 3 * b + 4)
                    sp.wait_ge(t_evD, 2 * b + 3)
                    sp.dma_start(tdram[:, ds(b, 1), :], tbuf[:, par:par + 1, :]).then_inc(t_stored[par], 16)

            def edges(L):
                if L.dedupe:
                    sp.wait_ge(acc_cleared, L.layer + 1)
                    for g in range(G):
                        sp.dma_start(L.acc[g][:, :].rearrange("(p n) w -> p (n w)", p=P),
                                     accT[:, 0:ACCN // P * L.width]).then_inc(L.acc_zeroed, 16)

                def load_ea(k, par):
                    c = 2 * k + par
                    sp.wait_ge(L.ea_ready, c + 1)
                    sp.dma_start(ea[:, par, :, :].rearrange("p (s g) w -> p s (g w)", g=G),
                                 by_tile_rows(t["edge_attr_16"])[:, ds(S * c, S), :]).then_inc(L.ea_in[par], 16)

                def body(k, par, last):
                    c = 2 * k + par
                    if L.layer == 1:
                        sp.wait_ge(L.ea_free, c + 1)
                        sp.dma_start(ea8[:, par, :, :].rearrange("p (s g) w -> p s (g w)", g=G),
                                     by_tile_rows(t["edge_attr_8"])[:, ds(S * c, S), :]).then_inc(L.ea_in[par], 16)
                    if L.layer == 3 and not last:
                        load_ea(k + par, 1 - par)
                    if not L.dedupe:
                        return
                    if L.pick:
                        _, bases = nc.values_load_multi_w_load_instructions(
                            base_i[0:1, ds(S * c, S + 1)], engines=[sp.engine], min_val=0, max_val=NP)
                    for j in range(S):
                        s, slot = S * c + j, slot_of(par, j)
                        sp.wait_ge(L.keys_free, s + 1)
                        sp.dma_start(keys[:, slot, :], L.key_dram[ds(s * P * G, P * G)].partition_broadcast(P))\
                          .then_inc(L.keys_in[slot], 16)
                        if L.pick:
                            sp.dma_start(drow[:, slot, :], t["dst"][ds(s * P * G, P * G)].partition_broadcast(P))\
                              .then_inc(L.keys_in[slot], 16)
                            sp.wait_ge(L.picked, s + 1)
                            sp.dma_start(ywin[:, slot, :], y_tab[ds(bases[j + 1], WIN), :]).then_inc(L.ywin_in[slot], 16)

                if L.layer == 3:
                    load_ea(0, 0)
                if L.dedupe or L.layer == 3:
                    run_chunks(sp, body)
                if L.dedupe:
                    w = L.width * NB
                    sp.wait_ge(L.loop_done, 1)
                    for g in range(4):
                        sp.dma_start(accT[:, g * w:(g + 1) * w], node_rows(L.acc[g])).then_inc(L.acc_loaded, 16)
                    sp.wait_ge(L.agg_done, 1)
                    sp.dma_start(accT[:, 0:w], node_rows(L.acc[4])).then_inc(L.acc_loaded, 16)

            sp.wait_ge(flag_ready, 1)
            either(sp, 0, edges)
            for g in range(NG):
                sp.wait_ge(product_used, SEQ["table1"] + g + 1)
                sp.dma_start(node_rows(y_tab)[:, g * GB * YW:(g + 1) * GB * YW],
                             gout[:, (g % 2) * GB * YW:(g % 2 + 1) * GB * YW]).then_inc(y_stored[g % 2], 16)
            sp.dma_start(y_tab[NP:NP + WIN, :], ones[:, :]).then_inc(table_stored, 16)
            for s in y_stored:
                sp.wait_ge(s, 16 * (NG // 2))
            sp.wait_ge(table_stored, 16)
            either(sp, 1, edges)
            sp.wait_ge(table_ready, 1)
            sp.dma_start(node_rows(z_tab), flat(big[:, :, :])).then_inc(table_stored, 16)
            either(sp, 2, edges)
            sp.wait_ge(table_ready, 2)
            sp.dma_start(node_rows(h_tab), flat(h_rows)).then_inc(table_stored, 16)
            either(sp, 3, edges)
            sp.wait_ge(out_ready, 1)
            sp.dma_start(out[0:full, :].rearrange("(p b) d -> p (b d)", b=NB), flat(x[0:last, :, :])).then_inc(out_stored, 16)
            sp.dma_start(out.rearrange("n d -> (n d)")[full * D:N * D].rearrange("(a n) -> a n", a=1),
                         flat(x[last:last + 1, 0:N - full, :])).then_inc(out_stored, 16)
            sp.wait_ge(out_stored, 32)

        @block.gpsimd
        def _(pool):
            pool.iota(iota_i[:, :], pattern=[[1, WIN]], base=0, channel_multiplier=0).then_inc(iota_done, 1)
            pool.iota(part_i[:, :], pattern=[[0, 1]], base=0, channel_multiplier=1).then_inc(iota_done, 1)
            pool.iota(mask_i[:, :], pattern=[[1, NB]], base=0, channel_multiplier=NB).then_inc(iota_done, 1)
            pool.iota(pow_i[:, 0:1], pattern=[[0, 1]], base=(127 + 63) << 23, channel_multiplier=-(1 << 23)).then_inc(iota_done, 1)
            pool.iota(pow_i[:, 1:2], pattern=[[0, 1]], base=(127 - 63) << 23, channel_multiplier=1 << 23).then_inc(iota_done, 1)
            pool.memset(ident[:, :], 0.0)
            pool.memset(ones[:, :], 1.0)
            pool.drain()
            pool.affine_select(out=ident[:, :], in_=ident[:, :], compare_op=ALU.not_equal, fill=1.0,
                               base=0, pattern=[[-1, P]], channel_multiplier=1)
            pool.affine_select(out=first_row[:, :], in_=ones[:, :], compare_op=ALU.is_equal, fill=0.0,
                               base=0, pattern=[[0, P]], channel_multiplier=1)
            pool.drain()
            pool.sem_inc(consts, 1)
            pool.wait_ge(range_ready, 1)
            pool.partition_all_reduce(range_all[:, :], range_in[:, :], P, MAX).then_inc(range_reduced, 1)

            def before_dma():
                pool.sem_inc(pool_turn, 1)

            def edges(L):
                def gather(k, par):
                    c = 2 * k + par
                    pool.wait_ge(L.idx_staged, c + 1)
                    pool.wait_ge(L.rows_free, c + 1)
                    before_dma()
                    o = rows3 if L.layer == 3 else rows
                    for i in range(TC):
                        pool.indirect_dma_start(o[:, par, i, :], None, L.table[:, :],
                                                bass.IndirectOffsetOnAxis(ap=ibuf[:, par, i:i + 1], axis=0))\
                            .then_inc(L.gathered[par], 16)

                def gather_y(k, par, j):
                    s, slot = S * (2 * k + par) + j, slot_of(par, j)
                    pool.wait_ge(L.idx_staged, 2 * k + par + 1)
                    pool.wait_ge(L.rows_free, s + 1)
                    before_dma()
                    for g in range(G):
                        pool.indirect_dma_start(yrow[:, slot, g, :], None, L.table[:, :],
                                                bass.IndirectOffsetOnAxis(ap=ibuf[:, par, G * j + g:G * j + g + 1], axis=0))\
                            .then_inc(L.gathered[slot], 16)

                def scatter(k, par, j):
                    s, slot = S * (2 * k + par) + j, slot_of(par, j)
                    pool.wait_ge(L.idx2_ready, s + 1)
                    pool.wait_ge(L.sums_taken, s + 3)
                    for g in range(G):
                        if not (isinstance(s, int) and s == 0):
                            pool.wait_ge(L.scattered[g], 16 * s)
                        if g == G - 1:
                            pool.sem_inc(L.slot_done, 1)
                        before_dma()
                        v = summed[:, slot, g * L.step:g * L.step + L.width]
                        pool.indirect_dma_start(L.acc[g][:, :], bass.IndirectOffsetOnAxis(ap=idx2[:, slot, g:g + 1], axis=0),
                                                v, None, compute_op=ALU.add).then_inc(L.scattered[g], 16)

                if L.dedupe:
                    pool.sem_inc(L.slot_done, 1)
                    pool.wait_ge(L.acc_zeroed, 16 * G)

                def body(k, par, last):
                    if L.layer == 1:
                        for j in range(S):
                            if L.gathers and not (last and j == S - 1):
                                nk, npar, nj = (k, par, j + 1) if j < S - 1 else (k + par, 1 - par, 0)
                                gather_y(nk, npar, nj)
                            scatter(k, par, j)
                        return
                    if L.window:
                        gather(k, par)
                        return
                    if not last:
                        gather(k + par, 1 - par)
                    for j in range(S):
                        scatter(k, par, j)

                if L.gathers:
                    pool.wait_ge(*{0: (t_stored[0], 16 * (NB // 2) + 16), 1: (flag_ready, 1),
                                   2: (table_stored, 32), 3: (table_stored, 48)}[L.layer])
                    if L.layer == 0:
                        pool.wait_ge(t_stored[1], 16 * (NB // 2) + 16)
                    if L.layer == 1:
                        for s in y_stored:
                            pool.wait_ge(s, 16 * (NG // 2))
                        gather_y(0, 0, 0)
                    elif L.dedupe:
                        gather(0, 0)
                run_chunks(pool, body, peel=L.dedupe)
                if L.dedupe:
                    for g in range(G):
                        pool.wait_ge(L.scattered[g], 16 * SUP)
                    pool.sem_inc(L.loop_done, 1)

            pool.wait_ge(flag_ready, 1)
            for layer in range(4):
                either(pool, layer, edges)

        @block.scalar
        def _(act):
            asked = [0]

            def fn(func, o, i, scale=1.0):
                asked[0] += 1
                act.wait_ge(fn_asked, asked[0])
                act.activation(o, i, func, scale=scale).then_inc(fn_done, 1)

            fn(ACT.Sqrt, nv[1][:, :], nv[0][:, :])
            act.wait_ge(cleared, 1)
            small_in = lambda o, i: act.dma_start(o, i).then_inc(weights_in, 16)
            for q, name in enumerate(("L0_gnn_loop_weight", "L1_gnn_W_msg_lin", "L1_gnn_W_upd_lin", None, "L3_gnn_root")):
                w = t["L3_gnn_b2"].rearrange("(i o) -> i o", o=D) if name is None else t[name]
                for b in range(GB):
                    small_in(wbd[D * b:D * b + D, q, D * b:D * b + D], w)
            for b in range(GB):
                small_in(ybd[D * b:D * b + D, YW * b:YW * (b + 1)], t["L1_gnn_W_msg_tp"].rearrange("i j h -> i (j h)"))
                small_in(ubd[D * b:D * b + D, 256 * b:256 * (b + 1)], t["L1_gnn_W_upd_tp"].rearrange("i h k -> i (h k)"))
            for b in range(4):
                small_in(w2bd[32 * b:32 * b + 32, D * b:D * b + D], t["L2_gnn_W2"])
            with nc.allow_non_contiguous_dma(reason="768 numbers, once"):
                small_in(wgT[:, :], t["L2_gnn_W_gcn"].rearrange("i k -> k i"))
            small_in(w1g[:, :], t["L2_gnn_W1"])
            for tile, name in ((b1g, "L2_gnn_b1"), (b2g, "L2_gnn_b2"), (bias3, "L3_gnn_bias"),
                               (gamma3, "L3_gnn_gamma"), (beta3, "L3_gnn_beta")):
                small_in(tile[:, :], t[name].partition_broadcast(P))
            for q in range(6):
                small_in(w1raw[D * q:D * q + D, :], t["L3_gnn_W1"])
            for q in range(3):
                small_in(w1raw[6 * D + q:6 * D + q + 1, :], t["L3_gnn_b1"].rearrange("(a n) -> a n", a=1))
            small_in(w2x[:, :, :], t["L3_gnn_W2"].rearrange("(a k) n -> k a n", a=2))
            act.wait_ge(wc_copied, 1)
            act.dma_start(wc_dram[:, :], wc[:, :]).then_inc(wc_stored, 16)
            act.wait_ge(wc_stored, 16)
            for b in range(GB):
                act.dma_start(cbd[D * b:D * b + D, 32 * b:32 * b + 32], wc_dram[:, :]).then_inc(cbd_in, 16)
            act.sem_inc(t_evA, 1)
            with act.Fori(0, NB // 2) as k:
                for par in range(2):
                    b = 2 * k + par
                    act.wait_ge(t_stored[par], 16 * k + 16)
                    for i in range(0, NPIECE, 2):
                        act.wait_ge(t_prod, NPIECE * b + i + 1)
                        act.activation(tbuf[:, par, i * PIECE:(i + 1) * PIECE].rearrange("p (a n) -> p a n", a=2),
                                       table_piece(par, i), ACT.Copy).then_inc(t_evA, 1)

            def ea_step_h(L, k, par):
                c = 2 * k + par
                act.wait_ge(L.ea_in[par], 16 * (k + 1))
                if not (isinstance(c, int) and c < 2):
                    act.wait_ge(L.ea_turned, S * (c - 1))
                x3 = ea[:, par, :, :]
                act.activation(ea_blocks(par, 0), x3.unsqueeze(2).to_broadcast([P, TC, 2, D]), ACT.Copy)
                act.activation(ea6[:, par, :, 5 * D:6 * D], x3, ACT.Copy)
                act.drain()
                act.sem_inc(L.ea_h, 1)

            def ea_step_m(L, k, par):
                act.wait_ge(L.ea_rest, 2 * (2 * k + par) + 1)
                act.activation(ea_blocks(par, 1), rest[:, :, :].unsqueeze(2).to_broadcast([P, TC, 2, D]), ACT.Copy)
                act.drain()
                act.sem_inc(L.ea_h, 1)

            def ea_step_l(L, k, par):
                act.wait_ge(L.ea_rest, 2 * (2 * k + par) + 2)
                act.activation(ea6[:, par, :, 4 * D:5 * D], rest[:, :, :], ACT.Copy).then_inc(L.ea_ready, 1)

            def edges(L):
                if L.dedupe:
                    act.sem_inc(L.sums_taken, 2)
                if L.layer == 3:
                    act.sem_inc(L.ea_ready, 2)
                    for step in (ea_step_h, ea_step_m, ea_step_l):
                        step(L, 0, 0)

                def copy_turned(s, slot):
                    act.wait_ge(L.ea_turned, s + 1)
                    act.activation(eaT[:, slot, :], ps[0:K6, 4, 0:G * P // 2].bitcast(BF16), ACT.Copy)\
                       .then_inc(L.ea_copied, 1)

                if L.in_parts:
                    copy_turned(0, 0)

                def body(k, par, last):
                    c = 2 * k + par
                    if L.layer == 0:
                        act.wait_ge(L.norm_asked, c + 1)
                        act.activation(sv[1][:, :], sv[0][:, :], ACT.Sqrt)
                        act.drain()
                        act.activation(sv[2][:, :], sv[1][:, :], ACT.Tanh, scale=SQC).then_inc(L.norm_done, 1)
                    for j in range(S):
                        s, slot = S * c + j, slot_of(par, j)
                        if L.layer == 1:
                            act.wait_ge(L.m_ready, s + 1)
                            act.wait_ge(L.sums_done, s + 1)
                            act.activation(mval[:, slot, :, 0:D], mpre[:, slot, :, :], ACT.Silu, scale=NORM_MSG)\
                               .then_inc(L.vals_ready, 1)
                        if L.layer == 3:
                            if not L.in_parts:
                                copy_turned(s, slot)
                            for g in range(G):
                                ts = (par + j + g) % 2
                                act.wait_ge(L.hid_done, G * s + g + 1)
                                act.activation(hid[:, ts, :], ps[:, ts, 0:256], ACT.Relu).then_inc(L.relu_done, 1)
                                if g == 0 and not last:
                                    {0: ea_step_h, 2: ea_step_m, 3: ea_step_l}.get(j, lambda *a: None)(L, k + par, 1 - par)
                                if g == 2 and L.in_parts and not (last and j == S - 1):
                                    copy_turned(s + 1, 1 - slot)
                                if g == 3 and L.in_parts:
                                    if j == 0:
                                        act.wait_ge(L.gathered[par], 16 * TC * (k + 1))
                                    act.wait_ge(L.sums_done, s + 1)
                                    act.activation(vparts[:, slot, :, :, D:VW],
                                                   parts3[:, par, G * j:G * j + G, 2 * D:5 * D].rearrange("p g (q w) -> p g q w", q=3),
                                                   ACT.Copy).then_inc(L.x_ready, 1)
                        if L.dedupe:
                            act.wait_ge(L.sums_done, s + 3)
                            act.wait_ge(L.slot_done, s + 1)
                            n = G * L.step + (0 if L.layer == 1 else G)
                            act.activation(summed[:, slot, 0:n], ps[:, 6 + slot, 0:n], ACT.Copy).then_inc(L.sums_taken, 1)

                if L.dedupe or L.layer in (0, 3):
                    run_chunks(act, body)

            act.wait_ge(flag_ready, 1)
            either(act, 0, edges)
            fn(ACT.Sqrt, nv[1][:, :], nv[0][:, :])
            fn(ACT.Sqrt, nv[1][:, :], nv[0][:, :])
            fn(ACT.Sqrt, nv[1][:, :], nv[0][:, :])
            fn(ACT.Tanh, nv[2][:, :], nv[1][:, :], SQC)
            fn(ACT.Sqrt, nv[1][:, :], nv[0][:, :])
            either(act, 1, edges)
            fn(ACT.Silu, big[:, :, :], big[:, :, :], NORM_UPD)
            fn(ACT.Sqrt, nv[1][:, :], nv[0][:, :])
            fn(ACT.Sqrt, nv[1][:, :], nv[0][:, :])
            either(act, 2, edges)
            fn(ACT.Sqrt, nv[1][:, :], nv[0][:, :])
            either(act, 3, edges)
            fn(ACT.Sqrt, bn[:, 3, :], bn[:, 2, :])

        @block.tensor
        def _(pe):
            pe.wait_ge(consts, 1)
            pe.wait_ge(base_asked, 1)
            for a, n in ((0, 512), (512, SUP - 512)):
                mm = pe.matmul(ps[:, a // 512, 0:n], first_row[:, :], rel[:, a:a + n, 0], start=True, stop=True)
            mm.then_inc(base_done, 1)
            pe.wait_ge(weights_in, 16 * WEIGHT_DMAS)
            pe.matmul(ps[0:D, 2, 0:32], wgT[:, :], w1g[:, :], start=True, stop=True).then_inc(wc_done, 1)

            def turn(par, n):
                pe.wait_ge(t_staged, n)
                pe.transpose(ps[0:K6, 6 + par, 0:P // 2].bitcast(BF16), stg[:, par, :], ident_b[:, :]).then_inc(t_turned, 1)

            def column(k, par, last):
                b = 2 * k + par
                if not last:
                    turn(1 - par, b + 2)
                pe.wait_ge(t_lhs, b + 1)
                free = ((t_evD, 2 * b + 1), (t_evA, 3 * b + 1), (t_evA, 3 * b + 2), (t_evD, 2 * b + 2), (t_evA, 3 * b + 3))
                for i in range(NPIECE):
                    pe.wait_ge(*free[i])
                    half = PIECE // 2
                    for a in range(2):
                        n0 = (2 * i + a) * half
                        mm = pe.matmul(table_piece(par, i)[:, a, :], lt[:, par, :], wt6[:, n0:n0 + half],
                                       start=True, stop=True)
                    mm.then_inc(t_prod, 1)

            turn(0, 1)
            with pe.Fori(0, NB // 2 - 1) as k:
                column(k, 0, False)
                column(k, 1, False)
            column(NB // 2 - 1, 0, False)
            column(NB // 2 - 1, 1, True)

            def sequence(name, lhs, rhs):
                base, n = SEQ[name], SEQ_COLS[name]
                pe.wait_ge(seq_ready, list(SEQ).index(name) + 1)

                def turn(g):
                    a = lhs(g)
                    pe.transpose(turn_out(g, a.shape[1]), a, ident[:, :]).then_inc(turned, 1)

                turn(0)
                for g in range(SEQ_GROUPS[name]):
                    if g + 1 < SEQ_GROUPS[name]:
                        turn(g + 1)
                    pe.wait_ge(turn_copied, base + g + 1)
                    if base + g + 1 - SEQ_SLOTS[name] > 0:
                        pe.wait_ge(product_used, base + g + 1 - SEQ_SLOTS[name])
                    kk = lhs(g).shape[1]
                    o = group_out(name, g)
                    w = xt[0:kk, g % 2, :]
                    if n < 448:
                        cols = min(n, rhs.shape[1]) if name != "gcn2" else kk // 2
                        mm = pe.matmul(o[:, 0:cols], w, rhs[0:kk, 0:cols], start=True, stop=True)
                    else:
                        for a in range(n // 448):
                            mm = pe.matmul(o[:, a, :], w, rhs[0:kk, 448 * a:448 * (a + 1)], start=True, stop=True)
                    mm.then_inc(product_done, 1)

            power = pow_i[:, 0:1].bitcast(F32)

            def group_of(a):
                return lambda g: flat(a[:, GB * g:GB * g + GB, :])

            def edges(L):
                pe.sem_inc(L.sums_done, 2)
                if L.pick:
                    pe.sem_inc(L.picked, 2)

                def window(k, par, j):
                    s, slot = S * (2 * k + par) + j, slot_of(par, j)
                    pe.wait_ge(L.matrix_ready, s + 1)
                    pe.wait_ge(L.vals_ready, s + 1)
                    pe.wait_ge(L.sums_taken, s + 1)
                    if L.in_parts:
                        pe.wait_ge(L.x_ready, s + 1)
                    for g in range(G):
                        if L.in_parts:
                            v, hot = vparts[:, slot, g, :, :].rearrange("p q w -> p (q w)"), onehot_b[:, slot, g, :]
                        else:
                            v, hot = vals[:, par, G * j + g, :], onehot[:, slot, g, :]
                        mm = pe.matmul(ps[0:v.shape[1], 6 + slot, 0:WIN], v, hot, start=(g == 0), stop=(g == G - 1))
                    mm.then_inc(L.sums_done, 1)

                def add_same(k, par, j):
                    s, slot = S * (2 * k + par) + j, slot_of(par, j)
                    pe.wait_ge(L.matrix_ready, s + 1)
                    pe.wait_ge(L.vals_ready, s + 1)
                    pe.wait_ge(L.sums_taken, s + 1)
                    for g in range(G):
                        v = mval[:, slot, g, :] if L.layer == 1 else vals[:, par, G * j + g, :]
                        a = g * L.step
                        mm = pe.matmul(ps[:, 6 + slot, a:a + L.step], same[:, slot, g, :], v, start=True, stop=True)
                        if L.layer != 1:
                            a = G * L.step + g
                            mm = pe.matmul(ps[:, 6 + slot, a:a + 1], same[:, slot, g, :], power, start=True, stop=True)
                    mm.then_inc(L.sums_done, 1)

                def pick(k, par, j):
                    s, slot = S * (2 * k + par) + j, slot_of(par, j)
                    pe.wait_ge(L.pick_ready, s + 1)
                    pe.wait_ge(L.ywin_in[slot], 16 * slot_count(k, par, j))
                    for g in range(G):
                        a = 1024 * slot + YW * g
                        mm = pe.matmul(psf[:, a:a + YW], picks[:, slot, g:G * P:G], ywin[:, slot, :], start=True, stop=True)
                    mm.then_inc(L.picked, 1)

                def turn_ea(k, par, j):
                    if j == 0:
                        pe.wait_ge(L.ea_ready, 2 * k + par + 3)
                    for q in range(G):
                        mm = pe.transpose(ps[0:K6, 4, q * P // 2:(q + 1) * P // 2].bitcast(BF16),
                                          ea6[:, par, G * j + q, :], ident_b[:, :])
                    mm.then_inc(L.ea_turned, 1)

                def hidden(k, par, i):
                    c, j, g = 2 * k + par, i // G, i % G
                    s, slot = S * c + j, slot_of(par, j)
                    if g == 0:
                        if not L.in_parts:
                            turn_ea(k, par, j)
                        pe.wait_ge(L.ea_copied, s + 1)
                    ts = (par + i) % 2
                    for a in range(2):
                        mm = pe.matmul(ps[:, ts, P * a:P * a + P], w1[:, P * a:P * a + P], eaT[:, slot, P * g:P * g + P],
                                       start=True, stop=True)
                    mm.then_inc(L.hid_done, 1)

                def edge_weights(k, par, i):
                    n = TC * (2 * k + par) + i
                    ts = (par + i) % 2
                    pe.wait_ge(L.relu_done, n + 1)
                    pe.wait_ge(L.w_used, n + 6 - W_AGO[i % G])
                    for a in range(2):
                        mm = pe.matmul(ps[:, W_BANK[i % G], 0:256], hid[:, ts, P * a:P * a + P], w2x[:, a, :],
                                       start=(a == 0), stop=(a == 1))
                    mm.then_inc(L.w_done, 1)

                reduce = window if L.window else add_same

                def body(k, par, last):
                    if L.in_parts:
                        for i in range(TC):
                            j, g = i // G, i % G
                            if g == 1 and j < S - 1:
                                turn_ea(k, par, j + 1)
                            elif g == 1 and not last:
                                turn_ea(k + par, 1 - par, 0)
                            if i < TC - 1:
                                hidden(k, par, i + 1)
                            elif not last:
                                hidden(k + par, 1 - par, 0)
                            edge_weights(k, par, i)
                            if g == 2 and j:
                                window(k, par, j - 1)
                            elif g == 2 and not (isinstance(k, int) and k + par == 0):
                                window(k - 1 + par, 1 - par, S - 1)
                    elif L.layer == 3:
                        hidden(k, par, 0)
                        for i in range(TC):
                            if (i + 1) % G:
                                hidden(k, par, i + 1)
                            edge_weights(k, par, i)
                            if i % G == G - 1:
                                reduce(k, par, i // G)
                                if i + 1 < TC:
                                    hidden(k, par, i + 1)
                    elif L.pick:
                        for j in range(S):
                            if j + 1 < S:
                                pick(k, par, j + 1)
                            elif not last:
                                pick(k + par, 1 - par, 0)
                            reduce(k, par, j)
                    else:
                        for j in range(S):
                            reduce(k, par, j)

                if L.pick:
                    pick(0, 0, 0)
                if L.in_parts:
                    turn_ea(0, 0, 0)
                    hidden(0, 0, 0)
                run_chunks(pe, body, peel=L.in_parts)
                if L.in_parts:
                    window(PAIRS, 0, S - 1)
                if L.window:
                    pe.wait_ge(L.sums_taken, SUP + 2)
                    for n in range(NB):
                        q, r = n // 14, n % 14
                        if r == 0 and q >= 2:
                            pe.wait_ge(L.agg_done, q - 1)
                        kk, turn = (3 * VW, fold[:, :]) if L.in_parts else (VW, ident[0:VW, 0:VW])
                        mm = pe.matmul(ps[:, q % 2, VW * r:VW * r + VW], accT[0:kk, n:n + NB * (P - 1) + 1:NB], turn,
                                       start=True, stop=True)
                        if r == 13:
                            mm.then_inc(L.loop_done, 1)

            pe.wait_ge(flag_ready, 1)
            either(pe, 0, edges)
            sequence("loop", group_of(htan), wbd[:, 0, :])
            sequence("table1", group_of(h), ybd[:, :])
            either(pe, 1, edges)
            sequence("msg_lin", group_of(big), wbd[:, 1, :])
            sequence("update", group_of(h), ubd[:, :])
            sequence("upd_lin", group_of(big), wbd[:, 2, :])
            pe.wait_ge(cbd_in, 16 * GB)
            either(pe, 2, edges)
            sequence("gcn1", group_of(big), cbd[:, :])
            sequence("gcn2", lambda g: flat(agg[:, 4 * g:min(4 * g + 4, NB), :]), w2bd[:, :])
            either(pe, 3, edges)
            sequence("bias_w", group_of(big), wbd[:, 3, :])
            sequence("root", group_of(h), wbd[:, 4, :])
            for n in range(2):
                pe.wait_ge(bn_asked, n + 1)
                pe.matmul(ps[:, n, 0:D], ones[:, :], bn[:, 2 * n, :], start=True, stop=True).then_inc(bn_done, 1)

        @block.vector
        def _(dve):
            tt, ts_, stt = dve.tensor_tensor, dve.tensor_scalar, dve.scalar_tensor_tensor
            asked = [0]

            def ask(ins=None):
                dve.drain()
                dve.sem_inc(fn_asked, 1)
                asked[0] += 1
                dve.wait_ge(fn_done, asked[0])

            def total(o, i, op=ALU.add):
                dve.tensor_reduce(o, i, AX.X, op)

            def each(v, d=D):
                return v.unsqueeze(2).to_broadcast([P, v.shape[1], d])

            def squares(o, i):
                tt(agg[:, :, 0:D], i, i, ALU.mult)
                dve.drain()
                total(o, agg[:, :, 0:D])
                dve.drain()

            def layer_norm():
                total(nv[0][:, :], x[:, :, :])
                dve.drain()
                ts_(nv[0][:, :], nv[0][:, :], 1.0 / D, None, ALU.mult)
                dve.drain()
                tt(h[:, :, :], x[:, :, :], each(nv[0][:, :]), ALU.subtract)
                dve.drain()
                squares(nv[0][:, :], h[:, :, :])
                ts_(nv[0][:, :], nv[0][:, :], 1.0 / D, LN_EPS, ALU.mult, ALU.add)
                ask()
                dve.reciprocal(nv[2][:, :], nv[1][:, :])
                dve.drain()
                tt(h[:, :, :], h[:, :, :], each(nv[2][:, :]), ALU.mult)
                dve.drain()
                ts_(h[:, :, :], h[:, :, :], 0.0, None, ALU.max)
                dve.drain()

            def clipped(o, i):
                ts_(o, i, MIN_NORM, None, ALU.max)

            dve.memset(x[:, :, :], 0.0)
            dve.memset(wbd[:, :, :], 0.0)
            for tile in (ybd, ubd, cbd, w2bd):
                dve.memset(tile[:, :], 0.0)
            dve.memset(ea6[:, :, :, :], 1.0)
            dve.drain()
            dve.sem_inc(cleared, 1)
            dve.wait_ge(iota_done, 5)
            dve.tensor_copy(iota[:, :], iota_i[:, :])
            dve.tensor_copy(part[:, :], part_i[:, :])
            ts_(junk[:, :], part_i[:, :], float(NP), None, ALU.add)
            ts_(mask[:, :], mask_i[:, :], float(N), None, ALU.is_lt)
            dve.wait_ge(consts, 1)
            dve.tensor_copy(ident_b[:, :], ident[:, :])
            tt(fold[:, :], ident[0:3 * VW, 0:VW], ident[0:3 * VW, VW:2 * VW], ALU.add)
            dve.drain()
            tt(fold[:, :], fold[:, :], ident[0:3 * VW, 2 * VW:3 * VW], ALU.add)
            for tile, letter, bias_row in ((in_h, "h", 0), (in_m, "m", 1), (in_l, "l", 2)):
                spans = [(D * q, D * q + D) for q in range(6) if RIGHT[q] == letter] + [(6 * D + bias_row, 6 * D + bias_row + 1)]
                for q, (lo, hi) in enumerate(spans):
                    ts_(band[0][:, q:q + 1], part[:, :], lo - 0.5, None, ALU.is_gt)
                    ts_(band[1][:, q:q + 1], part[:, :], hi - 0.5, None, ALU.is_lt)
                dve.drain()
                tt(band[0][:, 0:len(spans)], band[0][:, 0:len(spans)], band[1][:, 0:len(spans)], ALU.mult)
                dve.drain()
                total(tile[:, :], band[0][:, 0:len(spans)])
                dve.drain()

            def right_parts(o, w, a, b):
                dve.tensor_copy(a, w)
                dve.drain()
                tt(w, w, a, ALU.subtract)
                dve.drain()
                dve.tensor_copy(b, w)
                dve.drain()
                tt(w, w, b, ALU.subtract)
                ts_(o, a, in_h[0:K6, :], None, ALU.mult)
                dve.drain()
                stt(o, b, in_m[0:K6, :], o, ALU.mult, ALU.add)
                dve.drain()
                stt(o, w, in_l[0:K6, :], o, ALU.mult, ALU.add)
                dve.drain()

            def left_parts(x3, rest3, hm, mm_, l, h2):
                twice = [P, x3.shape[1], 2, D]
                dve.tensor_copy(hm, x3.unsqueeze(2).to_broadcast(twice))
                dve.tensor_copy(h2, x3)
                dve.drain()
                tt(rest3, x3, h2, ALU.subtract)
                dve.drain()
                dve.tensor_copy(mm_, rest3.unsqueeze(2).to_broadcast(twice))
                dve.drain()
                tt(rest3, rest3, mm_[:, :, 0, :], ALU.subtract)
                dve.drain()
                dve.tensor_copy(l, rest3)

            dve.wait_ge(x_in, 32)
            layer_norm()
            squares(nv[0][:, :], h[:, :, :])
            clipped(nv[0][:, :], nv[0][:, :])
            dve.drain()
            ts_(nv[0][:, :], nv[0][:, :], C, None, ALU.mult)
            dve.drain()
            ts_(nv[1][:, :], nv[0][:, :], 1.0 / (2 * ATANH_TERMS + 1), 1.0 / (2 * ATANH_TERMS - 1), ALU.mult, ALU.add)
            dve.drain()
            for n in range(ATANH_TERMS - 2, -1, -1):
                tt(nv[1][:, :], nv[1][:, :], nv[0][:, :], ALU.mult)
                dve.drain()
                ts_(nv[1][:, :], nv[1][:, :], 1.0 / (2 * n + 1), None, ALU.add)
                dve.drain()
            tt(htan[:, :, :], h[:, :, :], each(nv[1][:, :]), ALU.mult)
            dve.drain()

            blocks = htan6[:, :, 0:4 * D].rearrange("p b (a w) -> p b a w", a=2)
            dve.memset(htan6[:, :, 6 * D:K6], 1.0)
            left_parts(htan[:, :, :], big[:, :, :], blocks[:, :, :, 0:D], blocks[:, :, :, D:2 * D],
                       htan6[:, :, 4 * D:5 * D], htan6[:, :, 5 * D:6 * D])
            dve.wait_ge(rel_in, 16 * 9)
            right_parts(wt6, wt, accT[0:K6, 0:TROW // 2].bitcast(BF16), accT[0:K6, TROW // 2:TROW].bitcast(BF16))
            dve.wait_ge(weights_in, 16 * WEIGHT_DMAS)
            right_parts(w1[:, :], w1raw[:, :], accT[0:K6, 0:128].bitcast(BF16), accT[0:K6, 128:256].bitcast(BF16))

            dve.wait_ge(idx_in, 48)
            stt(tix[:, :, :], src[:, :, :], float(R), tix[:, :, :], ALU.mult, ALU.add)
            dve.tensor_copy(rel[:, :, :], dst[:, :, :])
            dve.drain()
            dve.sem_inc(base_asked, 1)
            dve.wait_ge(base_done, 1)
            dve.memset(base_i[:, 0:1], 0)
            dve.tensor_copy(base_i[:, 1:SUP + 1], psf[:, 0:SUP])
            ts_(base_p[:, :], psf[:, 0:SUP], part[:, 0:1], None, ALU.add)
            tt(rel[:, :, :], rel[:, :, :], psf[:, 0:SUP].unsqueeze(2).to_broadcast([P, SUP, G]), ALU.subtract)
            dve.drain()
            relf = rel[:, :, :].rearrange("p s g -> p (s g)")
            dve.tensor_reduce(range_in[:, 0:1], relf, AX.X, ALU.min, negate=True)
            dve.tensor_reduce(range_in[:, 1:2], relf, AX.X, ALU.max)
            dve.drain()
            dve.sem_inc(range_ready, 1)
            dve.wait_ge(range_reduced, 1)
            ts_(fits[:, 0:1], range_all[:, 0:1], 0.5, None, ALU.is_lt)
            ts_(fits[:, 1:2], range_all[:, 1:2], WIN - 0.5, None, ALU.is_lt)
            dve.drain()
            tt(flag[:, :], fits[:, 0:1], fits[:, 1:2], ALU.mult)
            dve.drain()
            dve.sem_inc(flag_ready, 1)
            dve.wait_ge(wc_done, 1)
            dve.tensor_copy(wc[:, :], ps[0:D, 2, 0:32]).then_inc(wc_copied, 1)

            def stage(par, b):
                dve.tensor_copy(stg[:, par, :].unsqueeze(1), htan6[:, ds(b, 1), :]).then_inc(t_staged, 1)
                dve.wait_ge(t_turned, b + 1)
                dve.tensor_copy(lt[:, par, :], ps[0:K6, 6 + par, 0:P // 2].bitcast(BF16)).then_inc(t_lhs, 1)

            def column(k, par, last):
                b = 2 * k + par
                if not last:
                    stage(1 - par, b + 1)
                dve.wait_ge(t_stored[par], 16 * k + 16)
                for i in range(1, NPIECE, 2):
                    dve.wait_ge(t_prod, NPIECE * b + i + 1)
                    dve.tensor_copy(tbuf[:, par, i * PIECE:(i + 1) * PIECE].rearrange("p (a n) -> p a n", a=2),
                                    table_piece(par, i)).then_inc(t_evD, 1)

            dve.sem_inc(t_evD, 1)
            stage(0, 0)
            with dve.Fori(0, NB // 2 - 1) as k:
                column(k, 0, False)
                column(k, 1, False)
            column(NB // 2 - 1, 0, False)
            column(NB // 2 - 1, 1, True)
            for s in t_stored:
                dve.wait_ge(s, 16 * (NB // 2) + 16)

            def edges(L):
                if L.gathers:
                    dve.sem_inc(L.rows_free, 2)
                if L.layer == 1:
                    dve.sem_inc(L.ea_free, 2)
                if L.window:
                    dve.sem_inc(L.sums_taken, 2)
                else:
                    dve.sem_inc(L.keys_free, 2)
                if L.layer == 3:
                    dve.sem_inc(L.w_used, 5)

                def stage_idx(k, par):
                    c = 2 * k + par
                    dve.tensor_copy(ibuf[:, par, :].rearrange("p (s g) -> p s g", g=G),
                                    L.idx[:, ds(S * c, S), :]).then_inc(L.idx_staged, 1)

                def onehots(k, par, j):
                    s, slot = S * (2 * k + par) + j, slot_of(par, j)
                    dve.wait_ge(L.sums_done, s + 1)
                    tt((onehot_b if L.in_parts else onehot)[:, slot, :, :], iota[:, :].unsqueeze(1).to_broadcast([P, G, WIN]),
                       rel[:, ds(s, 1), :].rearrange("p a g -> p (a g)").unsqueeze(2).to_broadcast([P, G, WIN]),
                       ALU.is_equal).then_inc(L.matrix_ready, 1)

                def base_before(s):
                    return dve.value_load(base_i[0:1, ds(s, 1)], min_val=0, max_val=NP)

                def add_window(k, par, j, base):
                    s, slot = S * (2 * k + par) + j, slot_of(par, j)
                    dve.wait_ge(L.sums_done, s + 3)
                    kk = 3 * VW if L.in_parts else VW
                    o = accT[0:kk, ds(base, WIN)]
                    tt(o, o, ps[0:kk, 6 + slot, 0:WIN], ALU.add)
                    dve.drain()
                    dve.sem_inc(L.sums_taken, 1)

                def compare(k, par, j):
                    s, slot = S * (2 * k + par) + j, slot_of(par, j)
                    dve.wait_ge(L.keys_in[slot], 16 * (2 if L.pick else 1) * slot_count(k, par, j))
                    if L.pick:
                        dve.wait_ge(L.picked, s + 1)
                        ts_(picks[:, slot, :], drow[:, slot, :], base_p[:, ds(s, 1)], None, ALU.is_equal)\
                            .then_inc(L.pick_ready, 1)
                    dve.wait_ge(L.sums_done, s + 1)
                    tt(same[:, slot, :, :], keys[:, slot, :].rearrange("p (e g) -> p g e", g=G),
                       key_of(s).unsqueeze(2).to_broadcast([P, G, P]), ALU.is_equal)
                    dve.drain()
                    dve.sem_inc(L.matrix_ready, 1)
                    dve.sem_inc(L.keys_free, 1)

                def key_of(s):
                    return L.key[:, ds(s, 1), :].rearrange("p a g -> p (a g)")

                def place(k, par, j):
                    s, slot = S * (2 * k + par) + j, slot_of(par, j)
                    dve.wait_ge(L.sums_taken, s + 3)
                    dve.wait_ge(L.slot_done, s + 1)
                    n = G * L.step
                    powers = summed[:, slot, D:n:D + 1] if L.layer == 1 else summed[:, slot, n:n + G]
                    ts_(cnt[:, :], powers, pow_i[:, 1:2].bitcast(F32), 2.5, ALU.mult, ALU.is_lt)
                    ts_(keyd[:, :], key_of(s), junk[:, 0:1], None, ALU.subtract)
                    dve.drain()
                    tt(keyd[:, :], cnt[:, :], keyd[:, :], ALU.mult)
                    dve.drain()
                    ts_(idx2[:, slot, :], keyd[:, :], junk[:, 0:1], None, ALU.add)
                    dve.drain()
                    dve.sem_inc(L.idx2_ready, 1)

                def values0(k, par):
                    m = rows[:, par, :, :]
                    v = vals[:, par, :, :]
                    sq = work[:, 0:TC * D].rearrange("p (t d) -> p t d", d=D)
                    n2, n, th, rn, f, q = (sv[i][:, :] for i in (3, 1, 2, 4, 5, 6))
                    tt(sq, m, m, ALU.mult)
                    dve.drain()
                    total(n2, sq)
                    dve.drain()
                    clipped(sv[0][:, :], n2)
                    dve.drain()
                    dve.sem_inc(L.norm_asked, 1)
                    dve.wait_ge(L.norm_done, 2 * k + par + 1)
                    dve.reciprocal(rn, n)
                    dve.drain()
                    stt(f, th, 1.0 / SQC, rn, ALU.mult, ALU.mult)
                    dve.drain()
                    tt(q, f, f, ALU.mult)
                    dve.drain()
                    tt(q, q, n2, ALU.mult)
                    dve.drain()
                    ts_(q, q, -C, 1.0, ALU.mult, ALU.add)
                    dve.drain()
                    ts_(q, q, EPS, None, ALU.add)
                    dve.drain()
                    dve.reciprocal(rn, q)
                    dve.drain()
                    ts_(v[:, :, D:D + 1].rearrange("p t a -> p (t a)"), rn, 2.0, None, ALU.mult)
                    stt(f, rn, 2.0, f, ALU.mult, ALU.mult)
                    dve.drain()
                    tt(v[:, :, 0:D], m, f.unsqueeze(2).to_broadcast([P, TC, D]), ALU.mult)
                    dve.drain()
                    dve.sem_inc(L.vals_ready, S)
                    dve.sem_inc(L.rows_free, 1)

                def values1(k, par, j):
                    s, slot = S * (2 * k + par) + j, slot_of(par, j)
                    if L.pick:
                        dve.wait_ge(L.picked, s + 3)
                        y = psf[:, 1024 * slot:1024 * slot + G * YW]
                    else:
                        dve.wait_ge(L.gathered[slot], 16 * G * slot_count(k, par, j))
                        y = yrow[:, slot, :, :].rearrange("p g w -> p (g w)")
                    w = work[:, 0:G * YW]
                    tt(w.rearrange("p (a h) -> p a h", h=D), y.rearrange("p (a h) -> p a h", h=D),
                       ea8[:, par, G * j:G * j + G, :].rearrange("p g j -> p (g j)").unsqueeze(2).to_broadcast([P, G * DE, D]),
                       ALU.mult)
                    dve.drain()
                    if L.gathers:
                        dve.sem_inc(L.rows_free, 1)
                    total(mpre[:, slot, :, :], w.rearrange("p (g j h) -> p g h j", j=DE, h=D))
                    dve.drain()
                    dve.sem_inc(L.m_ready, 1)
                    if j == S - 1:
                        dve.sem_inc(L.ea_free, 1)

                def values3(k, par, j, between=lambda g: None):
                    s, slot = S * (2 * k + par) + j, slot_of(par, j)
                    for g in range(G):
                        dve.wait_ge(L.w_done, G * s + g + 1)
                        tt(work[:, 256 * g:256 * g + 256].rearrange("p (i o) -> p i o", o=D),
                           ps[:, W_BANK[g], 0:256].rearrange("p (i o) -> p i o", o=D),
                           rows3[:, par, G * j + g, 0:D].unsqueeze(2).to_broadcast([P, D, D]), ALU.mult).then_inc(L.w_used, 1)
                        between(g)
                    dve.drain()
                    products = work[:, :].rearrange("p (g i o) -> p g o i", i=D, o=D)
                    if L.in_parts:
                        total(msg[:, :, :], products)
                        dve.drain()
                        dve.wait_ge(L.sums_done, s + 1)
                        v = [vparts[:, slot, :, q, 0:D] for q in range(3)]
                        dve.tensor_copy(v[0], msg[:, :, :])
                        dve.drain()
                        tt(msg[:, :, :], msg[:, :, :], v[0], ALU.subtract)
                        dve.drain()
                        dve.tensor_copy(v[1], msg[:, :, :])
                        dve.drain()
                        tt(v[2], msg[:, :, :], v[1], ALU.subtract).then_inc(L.vals_ready, 1)
                    else:
                        total(vals[:, par, G * j:G * j + G, 0:D], products)
                        dve.tensor_copy(vals[:, par, G * j:G * j + G, D:2 * D], rows3[:, par, G * j:G * j + G, 0:D])
                        dve.drain()
                        dve.sem_inc(L.vals_ready, 1)
                    if j == S - 1:
                        if L.in_parts:
                            dve.wait_ge(L.x_ready, S * (2 * k + par) + S)
                        dve.sem_inc(L.rows_free, 1)

                def ea_rest_h(k, par):
                    dve.wait_ge(L.ea_h, 2 * (2 * k + par) + 1)
                    tt(rest[:, :, :], ea[:, par, :, :], ea6[:, par, :, 0:D], ALU.subtract).then_inc(L.ea_rest, 1)

                def ea_rest_m(k, par):
                    dve.wait_ge(L.ea_h, 2 * (2 * k + par) + 2)
                    tt(rest[:, :, :], rest[:, :, :], ea6[:, par, :, D:2 * D], ALU.subtract).then_inc(L.ea_rest, 1)

                def body(k, par, last):
                    c = 2 * k + par
                    if L.gathers and not last:
                        stage_idx(k + par, 1 - par)
                    if L.window and not L.in_parts:
                        _, bases = nc.values_load_multi_w_load_instructions(
                            base_i[0:1, ds(S * c, S + 1)], engines=[dve.engine], min_val=0, max_val=NP)
                    if L.layer == 1:
                        dve.wait_ge(L.ea_in[par], 16 * (k + 1))
                    else:
                        dve.wait_ge(L.gathered[par], 16 * TC * (k + 1))
                    if L.layer == 0:
                        values0(k, par)
                    if L.layer == 2:
                        dve.tensor_copy(vals[:, par, :, 0:D], rows[:, par, :, :])
                        dve.drain()
                        dve.sem_inc(L.vals_ready, S)
                        dve.sem_inc(L.rows_free, 1)
                    for j in range(S if L.in_parts else 0):
                        def between(g):
                            if g == 0:
                                onehots(k, par, j)
                            if g == 3 and j:
                                add_window(k, par, j - 1, base_before(S * c + j))
                            elif g == 3 and not (isinstance(k, int) and k + par == 0):
                                add_window(k - 1 + par, 1 - par, S - 1, base_before(S * c))
                            if g == 2 and not last and j in (1, 2):
                                (ea_rest_h if j == 1 else ea_rest_m)(k + par, 1 - par)

                        values3(k, par, j, between)
                    if L.in_parts:
                        return
                    for j in range(S):
                        if L.window:
                            onehots(k, par, j)
                        elif L.layer != 1:
                            compare(k, par, j)
                        elif j < S - 1:
                            compare(k, par, j + 1)
                        elif not last:
                            compare(k + par, 1 - par, 0)
                        if L.layer == 1:
                            values1(k, par, j)
                            if j:
                                place(k, par, j - 1)
                            elif not (isinstance(c, int) and c == 0):
                                place(k - 1 + par, 1 - par, S - 1)
                        if L.layer == 3:
                            values3(k, par, j)
                            if not last and j in (1, 2):
                                (ea_rest_h if j == 1 else ea_rest_m)(k + par, 1 - par)
                        if L.dedupe and L.layer != 1:
                            place(k, par, j)
                        if L.window and j:
                            add_window(k, par, j - 1, bases[j])
                    if L.window:
                        add_window(k, par, S - 1, bases[S])

                if L.gathers:
                    stage_idx(0, 0)
                if L.layer == 1:
                    compare(0, 0, 0)
                if L.layer == 3:
                    ea_rest_h(0, 0)
                    ea_rest_m(0, 0)
                run_chunks(dve, body, peel=L.layer == 1 or L.in_parts)
                if L.in_parts:
                    add_window(PAIRS, 0, S - 1, base_before(SUP))
                if L.layer == 1:
                    place(PAIRS, 0, S - 1)

                if L.window:
                    for q in range(NB // 14):
                        dve.wait_ge(L.loop_done, q + 1)
                        dve.tensor_copy(flat(agg[:, 14 * q:14 * q + 14, :]), ps[:, q % 2, 0:14 * VW]).then_inc(L.agg_done, 1)
                    dve.drain()
                else:
                    w = L.width * NB
                    o = agg[:, :, 0:L.width]
                    parts = [accT[:, i * w:(i + 1) * w].rearrange("p (b w) -> p b w", b=NB) for i in range(4)]
                    dve.wait_ge(L.acc_loaded, 64)
                    tt(o, parts[0], parts[1], ALU.add)
                    dve.drain()
                    tt(o, o, parts[2], ALU.add)
                    dve.drain()
                    tt(o, o, parts[3], ALU.add)
                    dve.drain()
                    dve.sem_inc(L.agg_done, 1)
                    dve.wait_ge(L.acc_loaded, 80)
                    tt(o, o, parts[0], ALU.add)
                    dve.drain()

            def begin_edges():
                dve.memset(accT[:, :], 0.0)
                dve.drain()
                dve.sem_inc(acc_cleared, 1)

            def sequence(name, lhs_cols, use):
                base = SEQ[name]
                dve.drain()
                dve.sem_inc(seq_ready, 1)

                def copy(g):
                    dve.wait_ge(turned, base + g + 1)
                    dve.tensor_copy(xt[0:lhs_cols(g), g % 2, :], turn_out(g, lhs_cols(g))).then_inc(turn_copied, 1)

                copy(0)
                for g in range(SEQ_GROUPS[name]):
                    if g + 1 < SEQ_GROUPS[name]:
                        copy(g + 1)
                    dve.wait_ge(product_done, base + g + 1)
                    use(g, group_out(name, g))
                    dve.drain()
                    dve.sem_inc(product_used, 1)
                dve.drain()

            cols7 = lambda g: GB * D

            def into(tile, scale=1.0, add=None):
                def use(g, o):
                    dest = flat(tile[:, GB * g:GB * g + GB, :])
                    if add is None:
                        ts_(dest, o, scale, None, ALU.mult)
                    else:
                        stt(dest, o, scale, flat(add[:, GB * g:GB * g + GB, :]), ALU.mult, ALU.add)
                return use

            begin_edges()
            dve.memset(vals[:, :, :, :], 0.0)
            dve.drain()
            for par in range(2):
                dve.memset(vals[:, par, :, D + 1:D + 2], 1.0)
            dve.drain()
            either(dve, 0, edges)

            one_over = dve.reciprocal
            dve.tensor_copy(deg[:, :], agg[:, :, D + 1:D + 2].rearrange("p b a -> p (b a)"))
            dve.drain()
            ts_(nv[0][:, :], deg[:, :], 1.0, None, ALU.max)
            ask()
            one_over(nv[2][:, :], nv[1][:, :])
            dve.drain()
            tt(nv[3][:, :], deg[:, :], nv[2][:, :], ALU.mult)
            dve.drain()
            ts_(nv[3][:, :], nv[3][:, :], EPS, None, ALU.add)
            dve.drain()
            one_over(nv[4][:, :], nv[3][:, :])
            dve.drain()
            tt(nv[2][:, :], nv[2][:, :], nv[4][:, :], ALU.mult)
            dve.drain()
            tt(nv[3][:, :], nv[2][:, :], agg[:, :, D:D + 1].rearrange("p b a -> p (b a)"), ALU.mult)
            dve.drain()
            ts_(nv[3][:, :], nv[3][:, :], EPS, None, ALU.add)
            dve.drain()
            one_over(nv[4][:, :], nv[3][:, :])
            dve.drain()
            tt(nv[2][:, :], nv[2][:, :], nv[4][:, :], ALU.mult)
            dve.drain()
            tt(big[:, :, :], agg[:, :, 0:D], each(nv[2][:, :]), ALU.mult)
            dve.drain()
            squares(nv[0][:, :], big[:, :, :])
            clipped(nv[0][:, :], nv[0][:, :])
            ask()
            one_over(nv[2][:, :], nv[1][:, :])
            dve.drain()
            ts_(nv[2][:, :], nv[2][:, :], (1.0 - BALL_EPS) / SQC, 1.0, ALU.mult, ALU.min)
            dve.drain()
            tt(big[:, :, :], big[:, :, :], each(nv[2][:, :]), ALU.mult)
            sequence("loop", cols7, into(htan))
            squares(nv[0][:, :], htan[:, :, :])
            clipped(nv[0][:, :], nv[0][:, :])
            ask()
            ask()
            one_over(nv[3][:, :], nv[1][:, :])
            dve.drain()
            stt(nv[3][:, :], nv[2][:, :], 1.0 / SQC, nv[3][:, :], ALU.mult, ALU.mult)
            dve.drain()
            tt(htan[:, :, :], htan[:, :, :], each(nv[3][:, :]), ALU.mult)
            dve.drain()
            x2, y2, xy, a, b, den = (v[:, :] for v in nv)
            squares(x2, big[:, :, :])
            squares(y2, htan[:, :, :])
            tt(agg[:, :, 0:D], big[:, :, :], htan[:, :, :], ALU.mult)
            dve.drain()
            total(xy, agg[:, :, 0:D])
            dve.drain()
            ts_(xy, xy, 2 * C, 1.0, ALU.mult, ALU.add)
            ts_(b, x2, -C, 1.0, ALU.mult, ALU.add)
            tt(den, x2, y2, ALU.mult)
            dve.drain()
            stt(a, y2, C, xy, ALU.mult, ALU.add)
            stt(den, den, C * C, xy, ALU.mult, ALU.add)
            dve.drain()
            ts_(den, den, MIN_NORM, None, ALU.max)
            tt(big[:, :, :], big[:, :, :], each(a), ALU.mult)
            tt(htan[:, :, :], htan[:, :, :], each(b), ALU.mult)
            dve.drain()
            one_over(x2, den)
            tt(big[:, :, :], big[:, :, :], htan[:, :, :], ALU.add)
            dve.drain()
            tt(big[:, :, :], big[:, :, :], each(x2), ALU.mult)
            dve.drain()
            tt(x[:, :, :], x[:, :, :], big[:, :, :], ALU.add)
            dve.drain()

            layer_norm()

            def to_table(g, o):
                if g >= 2:
                    dve.wait_ge(y_stored[g % 2], 16 * (g // 2))
                dve.tensor_copy(gout[:, (g % 2) * 896:(g % 2 + 1) * 896].rearrange("p (a n) -> p a n", a=2), o)

            sequence("table1", cols7, to_table)
            for s in y_stored:
                dve.wait_ge(s, 16 * (NG // 2))
            begin_edges()
            dve.tensor_copy(mval[:, :, :, D:D + 1].rearrange("p a g w -> p (a g w)"),
                            pow_i[:, 0:1].bitcast(F32).to_broadcast([P, 2 * G]))
            dve.drain()
            either(dve, 1, edges)
            dve.tensor_copy(big[:, :, :], agg[:, :, 0:D])
            sequence("msg_lin", cols7, into(htan, NORM_LIN))

            def update(g, o):
                s = htan[:, GB * g:GB * g + GB, :].rearrange("p b h -> p (b h)")
                w = gout[:, :]
                for q in range(4):
                    tt(w[:, 448 * q:448 * (q + 1)].rearrange("p (a k) -> p a k", k=D),
                       o[:, q, :].rearrange("p (a k) -> p a k", k=D),
                       s[:, 28 * q:28 * (q + 1)].unsqueeze(2).to_broadcast([P, 28, D]), ALU.mult)
                dve.drain()
                total(big[:, GB * g:GB * g + GB, :], w.rearrange("p (b h k) -> p b k h", h=D, k=D))

            sequence("update", cols7, update)
            ask()
            sequence("upd_lin", cols7, into(htan, NORM_LIN, h))
            tt(x[:, :, :], x[:, :, :], htan[:, :, :], ALU.add)
            dve.drain()

            layer_norm()
            ts_(nv[0][:, :], deg[:, :], 1.0, None, ALU.add)
            ask()
            one_over(deg[:, :], nv[1][:, :])
            dve.drain()
            tt(big[:, :, :], h[:, :, :], each(deg[:, :]), ALU.mult)
            dve.drain()
            dve.sem_inc(table_ready, 1)
            begin_edges()
            dve.memset(vals[:, :, :, :], 0.0)
            dve.drain()
            either(dve, 2, edges)
            tt(big[:, :, :], big[:, :, :], agg[:, :, 0:D], ALU.add)
            dve.drain()
            tt(big[:, :, :], big[:, :, :], each(deg[:, :]), ALU.mult)

            def relu_bias(g, o):
                hidden = agg[:, GB * g:GB * g + GB, :]
                tt(hidden, o.rearrange("p (b k) -> p b k", b=GB), b1g[:, :].unsqueeze(1).to_broadcast([P, GB, 32]), ALU.add)
                dve.drain()
                ts_(hidden, hidden, 0.0, None, ALU.max)

            sequence("gcn1", cols7, relu_bias)

            def residual(g, o):
                n = min(4, NB - 4 * g)
                tt(htan[:, 4 * g:4 * g + n, :], o[:, 0:n * D].rearrange("p (b k) -> p b k", k=D),
                   b2g[:, :].unsqueeze(1).to_broadcast([P, n, D]), ALU.add)

            sequence("gcn2", lambda g: 32 * min(4, NB - 4 * g), residual)
            tt(htan[:, :, :], htan[:, :, :], h[:, :, :], ALU.add)
            dve.drain()
            tt(x[:, :, :], x[:, :, :], htan[:, :, :], ALU.add)
            dve.drain()

            layer_norm()
            dve.tensor_copy(h_rows[:, :, 0:D], h[:, :, :])
            part3 = [h_parts[:, :, (2 + q) * D:(3 + q) * D] for q in range(3)]
            dve.tensor_copy(part3[0], h[:, :, :])
            dve.drain()
            tt(big[:, :, :], h[:, :, :], part3[0], ALU.subtract)
            dve.drain()
            dve.tensor_copy(part3[1], big[:, :, :])
            dve.drain()
            tt(big[:, :, :], big[:, :, :], part3[1], ALU.subtract)
            dve.drain()
            dve.tensor_copy(part3[2], big[:, :, :])
            dve.drain()
            dve.sem_inc(table_ready, 1)
            dve.wait_ge(table_stored, 48)
            begin_edges()
            either(dve, 3, edges)
            dve.tensor_copy(htan[:, :, :], agg[:, :, 0:D])
            dve.tensor_copy(big[:, :, :], agg[:, :, D:2 * D])
            sequence("bias_w", cols7, into(htan, 1.0, htan))
            sequence("root", cols7, into(big, 1.0, htan))
            tt(big[:, :, :], big[:, :, :], bias3[:, :].unsqueeze(1).to_broadcast([P, NB, D]), ALU.add)
            dve.drain()

            def batch_sum(n, i):
                tt(htan[:, :, :], i, each(mask[:, :]), ALU.mult)
                dve.drain()
                total(bn[:, 2 * n, :], htan[:, :, :].rearrange("p b d -> p d b"))
                dve.drain()
                dve.sem_inc(bn_asked, 1)
                dve.wait_ge(bn_done, n + 1)
                ts_(bn[:, 1, :], ps[:, n, 0:D], 1.0 / N, None, ALU.mult)
                dve.drain()

            def every(v):
                return v.unsqueeze(1).to_broadcast([P, NB, D])

            batch_sum(0, big[:, :, :])
            tt(big[:, :, :], big[:, :, :], every(bn[:, 1, :]), ALU.subtract)
            dve.drain()
            tt(h[:, :, :], big[:, :, :], big[:, :, :], ALU.mult)
            dve.drain()
            batch_sum(1, h[:, :, :])
            ts_(bn[:, 2, :], bn[:, 1, :], LN_EPS, None, ALU.add)
            ask()
            dve.reciprocal(bn[:, 4, :], bn[:, 3, :])
            dve.drain()
            tt(bn[:, 4, :], bn[:, 4, :], gamma3[:, :], ALU.mult)
            dve.drain()
            tt(big[:, :, :], big[:, :, :], every(bn[:, 4, :]), ALU.mult)
            dve.drain()
            tt(big[:, :, :], big[:, :, :], every(beta3[:, :]), ALU.add)
            dve.drain()
            stt(x[:, :, :], big[:, :, :], 0.0, x[:, :, :], ALU.max, ALU.add)
            dve.drain()
            dve.sem_inc(out_ready, 1)


_INS = ["x", "src", "dst", "edge_attr_16", "edge_attr_8", "edge_type_230", "node_vec1",
        "L0_gnn_rel_weight", "L0_gnn_loop_weight", "L0_gnn_rel_emb",
        "L1_gnn_W_msg_tp", "L1_gnn_W_msg_lin", "L1_gnn_W_upd_tp", "L1_gnn_W_upd_lin",
        "L2_gnn_W_gcn", "L2_gnn_W1", "L2_gnn_b1", "L2_gnn_W2", "L2_gnn_b2",
        "L3_gnn_W1", "L3_gnn_b1", "L3_gnn_W2", "L3_gnn_b2", "L3_gnn_root", "L3_gnn_bias",
        "L3_gnn_gamma", "L3_gnn_beta"]


def kernel(**inputs):
    import numpy as _np
    import concourse.bacc as _bacc
    from concourse import mybir as _mybir
    from concourse.bass_utils import run_bass_kernel_spmd as _run

    nc = _bacc.Bacc("TRN2", target_bir_lowering=False, num_devices=1)
    arrays, args = {}, {}
    for name in _INS:
        a = _np.ascontiguousarray(inputs[name])
        arrays[f"in_{name}"] = a
        args[name] = nc.dram_tensor(f"in_{name}", a.shape, _mybir.dt.from_np(a.dtype), kind="ExternalInput").ap()
    out = nc.dram_tensor("out_x", (N, D), F32, kind="ExternalOutput").ap()
    gnn_kernel(nc, args, out)
    r = _run(nc, [arrays], core_ids=[0])
    return r.results[0]["out_x"]
```
